# Optimizing a Trainium2 kernel written in Bass

```python
import numpy as np
import jax
import jax.numpy as jnp

def _softmax(x, axis=-1):
    return jax.nn.softmax(x, axis=axis)

def _gelu(x):
    return jax.nn.gelu(x, approximate=True)

def _silu(x):
    return jax.nn.silu(x)

def _sigmoid(x):
    return jax.nn.sigmoid(x)

def _layernorm(x, axis=-1, eps=1e-05):
    m = jnp.mean(x, axis=axis, keepdims=True)
    v = jnp.var(x, axis=axis, keepdims=True)
    return (x - m) / jnp.sqrt(v + eps)

def _scatter_add(tgt, idx, src, axis=0):
    return tgt.at[idx].add(src)

def _segment_sum(src, seg, n):
    return jax.ops.segment_sum(src, seg, n)
kernel_name = 'mk_adaln_ffn_d1_seqx_r4_e369a4'

def setup_inputs(seed: int=0):
    np.random.seed(seed)
    _w = jnp.asarray

    def _rec_inputs():
        import jax
        import jax.numpy as jnp
        _rk = jax.random.key(seed)
        x = -0.000125 + 0.9999 * jax.random.normal(jax.random.fold_in(_rk, 1), (4, 512, 512), jnp.float32)
        _lenS = 512 - jax.random.randint(jax.random.fold_in(_rk, 7), (4,), 0, max(1, 512 // 4) + 1, jnp.int32)
        _lenS2 = 512 - jax.random.randint(jax.random.fold_in(_rk, 8), (4,), 0, max(1, 512 // 4) + 1, jnp.int32)
        itok_B_0_3 = jax.random.randint(jax.random.fold_in(_rk, 11), (4,), 0, 4, jnp.int32)
        return (x, itok_B_0_3)
    x, itok_B_0_3 = _rec_inputs()

    def _L0_cond_setup():
        import jax, jax.numpy as jnp
        import numpy as np
        B, S, D_IN, D_OUT, R, E = (8, 512, 512, 512, 16, 4)
        key = jax.random.key(seed)
        ks = jax.random.split(key, 7)
        x = jax.random.normal(ks[0], (B, S, D_IN), dtype=jnp.float32)
        W_base = jax.random.normal(ks[1], (D_OUT, D_IN), dtype=jnp.float32) * 0.02
        Wt = jax.random.normal(ks[2], (D_IN, D_IN), dtype=jnp.float32) * 0.02
        A = jax.random.normal(ks[3], (E, R, D_IN), dtype=jnp.float32) * 0.02
        B_w = jax.random.normal(ks[4], (E, D_OUT, R), dtype=jnp.float32) * 0.02
        Wp = jax.random.normal(ks[5], (D_OUT, D_OUT), dtype=jnp.float32) * 0.02
        scaling = jnp.ones((E,), dtype=jnp.float32)
        adapter_idx = jax.random.randint(ks[6], (B,), 0, E)
        return {'x': x, 'W_base': W_base, 'Wt': Wt, 'A': A, 'B_w': B_w, 'Wp': Wp, 'scaling': scaling, 'adapter_idx': adapter_idx}
    _L0_cond_all = _L0_cond_setup()
    _L0_cond_in = {k: v for k, v in _L0_cond_all.items() if k in ('W_base', 'Wt', 'A', 'B_w', 'Wp', 'scaling')}
    del _L0_cond_all

    def _L0_ffn_setup():
        import jax, jax.numpy as jnp
        import numpy as np
        HIDDEN = 512
        INTER = 352
        NUM_EXPERTS = 16
        TOP_K = 2
        BATCH, SEQ = (2, 512)
        key = jax.random.key(seed)
        ks = jax.random.split(key, 5)
        scale_h = 1.0 / np.sqrt(HIDDEN)
        scale_i = 1.0 / np.sqrt(INTER)
        return {'hidden_states': jax.random.normal(ks[0], (BATCH, SEQ, HIDDEN), jnp.float32), 'gate_w': jax.random.normal(ks[1], (NUM_EXPERTS, HIDDEN), jnp.float32) * scale_h, 'w_gate': jax.random.normal(ks[2], (NUM_EXPERTS, INTER, HIDDEN), jnp.float32) * scale_h, 'w_up': jax.random.normal(ks[3], (NUM_EXPERTS, INTER, HIDDEN), jnp.float32) * scale_h, 'w_down': jax.random.normal(ks[4], (NUM_EXPERTS, HIDDEN, INTER), jnp.float32) * scale_i}
    _L0_ffn_all = _L0_ffn_setup()
    _L0_ffn_in = {k: v for k, v in _L0_ffn_all.items() if k in ('gate_w', 'w_gate', 'w_up', 'w_down')}
    del _L0_ffn_all
    return {'x': x, 'itok_B_0_3': itok_B_0_3, 'L0_cond_W_base': _L0_cond_in['W_base'], 'L0_cond_Wt': _L0_cond_in['Wt'], 'L0_cond_A': _L0_cond_in['A'], 'L0_cond_B_w': _L0_cond_in['B_w'], 'L0_cond_Wp': _L0_cond_in['Wp'], 'L0_cond_scaling': _L0_cond_in['scaling'], 'L0_ffn_gate_w': _L0_ffn_in['gate_w'], 'L0_ffn_w_gate': _L0_ffn_in['w_gate'], 'L0_ffn_w_up': _L0_ffn_in['w_up'], 'L0_ffn_w_down': _L0_ffn_in['w_down']}

def reference(x, itok_B_0_3, L0_cond_W_base, L0_cond_Wt, L0_cond_A, L0_cond_B_w, L0_cond_Wp, L0_cond_scaling, L0_ffn_gate_w, L0_ffn_w_gate, L0_ffn_w_up, L0_ffn_w_down):
    import jax
    import jax.numpy as jnp

    def _L0_cond_ref(x, W_base, Wt, A, B_w, Wp, scaling, adapter_idx):
        import jax, jax.numpy as jnp
        import numpy as np
        B, S, D_IN, D_OUT, R, E = (8, 512, 512, 512, 16, 4)
        base = jnp.einsum('bsi,oi->bso', x, W_base)
        h = jnp.einsum('bsi,ji->bsj', x, Wt)
        Ab = A[adapter_idx]
        Bb = B_w[adapter_idx]
        sc = scaling[adapter_idx]
        z = jnp.einsum('bsj,brj->bsr', h, Ab)
        l = jnp.einsum('bsr,bor->bso', z, Bb)
        lora_out = jnp.einsum('bso,po->bsp', l, Wp) * sc[:, None, None]
        return base + lora_out

    def _L0_ffn_ref(hidden_states, gate_w, w_gate, w_up, w_down):
        import jax, jax.numpy as jnp
        import numpy as np
        HIDDEN = 512
        INTER = 352
        NUM_EXPERTS = 16
        TOP_K = 2
        BATCH, SEQ = (2, 512)
        B, S, H = hidden_states.shape
        E = gate_w.shape[0]
        x = hidden_states.reshape(-1, H)
        T = x.shape[0]
        logits = jnp.dot(x.astype(jnp.float32), gate_w.astype(jnp.float32).T)
        probs = jax.nn.softmax(logits, axis=-1)
        topk_w, topk_idx = jax.lax.top_k(probs, TOP_K)
        topk_w = topk_w / (jnp.sum(topk_w, axis=-1, keepdims=True) + 1e-20)
        combine = jnp.zeros((T, E), dtype=x.dtype).at[jnp.arange(T)[:, None], topk_idx].add(topk_w.astype(x.dtype))
        g = jnp.einsum('th,eih->tei', x, w_gate)
        u = jnp.einsum('th,eih->tei', x, w_up)
        h = jax.nn.silu(g) * u
        expert_out = jnp.einsum('tei,ehi->teh', h, w_down)
        y = jnp.einsum('te,teh->th', combine, expert_out)
        return y.reshape(B, S, H)
    x = x + _L0_ffn_ref(_L0_cond_ref(x, L0_cond_W_base, L0_cond_Wt, L0_cond_A, L0_cond_B_w, L0_cond_Wp, L0_cond_scaling, itok_B_0_3), L0_ffn_gate_w, L0_ffn_w_gate, L0_ffn_w_up, L0_ffn_w_down)
    return x

_drawn_inputs = setup_inputs


def setup_inputs(seed=0):
    import zlib

    import numpy as np

    out = dict(_drawn_inputs(seed))
    spreads = {'L0_cond_scaling': (1.0, 0.6)}
    factors = {'L0_cond_Wt': 4.124, 'L0_cond_A': 4.3, 'L0_cond_B_w': 4.162, 'L0_cond_Wp': 4.211}
    for name, (base, spread) in spreads.items():
        noise = np.random.default_rng([zlib.crc32(name.encode()), seed]).standard_normal(out[name].shape)
        drawn = base * np.exp(spread * noise) if base else spread * noise
        out[name] = jnp.asarray(drawn.astype(out[name].dtype))
    for name, factor in factors.items():
        out[name] = (out[name] * factor).astype(out[name].dtype)
    return out
```

```python
from contextlib import ExitStack, contextmanager

import concourse.bass as bass
from concourse import mybir

P = 128
F32 = mybir.dt.float32
F32R = mybir.dt.float32r
BF16 = mybir.dt.bfloat16
I32 = mybir.dt.int32
U32 = mybir.dt.uint32
ALU = mybir.AluOpType
ACT = mybir.ActivationFunctionType
AX_X = mybir.AxisListType.X

NBATCH, SEQ, H = 4, 512, 512
NADAPT, RANK = 4, 16
NEXP, INTER, TOPK = 16, 352, 2
NTOK = NBATCH * SEQ
KH = H // P
RR = NADAPT * RANK
CH = NTOK // P
CPB = CH // NBATCH
NSEL = CH * TOPK
KI = -(-INTER // P)
ILAST = INTER - (KI - 1) * P
NTILE = (NTOK * TOPK + NEXP * (P - 1)) // P
NFULL = NTOK * TOPK // P
TQ = 48
GU = 2 * INTER
GUW = KH * GU
DW = KI * H
EW = GUW + DW
NRAW, NSPLIT = 2, 3
NXG, NYS = 4, 3
SKIP = 4096

C_ID, C_IQ, C_TOK, C_ADP, CW = 0, P, P + TQ, P + TQ + CH, P + TQ + CH + 1
R_TRI, R_ONE, R_REV, R_THR, R_CUM, R_TH3, R_IM, RW = 0, P, 2 * P, 2 * P + 16, 2 * P + 32, 2 * P + 288, 2 * P + 293, 3 * P + 293


def build(nc, cst, rcst, small, adp, scl, wt, wpt, wb, wbt, xt, x, wall, out):
    with ExitStack() as ctx:
        sem_names = []

        def sem(name):
            sem_names.append(name)
            return ctx.enter_context(nc.semaphore(name))

        arena0 = -(-nc.sbuf_base // 64) * 64
        arena_size = nc.sbuf_usable_end // 64 * 64 - arena0

        def region(start, size):
            at = [start]

            def place(name, shape, dt):
                nbytes = 2 if dt == BF16 else 4
                for s in shape[1:]:
                    nbytes *= s
                nbytes = -(-nbytes // 32) * 32
                assert at[0] + nbytes <= start + size, (name, at[0] + nbytes - start - size)
                t = nc.alloc_sbuf_tensor_at(name, shape, dt, offset=arena0 + at[0])
                at[0] += nbytes
                return t
            return place

        SLOT = EW * 4
        o_hi, o_lo, o_raw = 0, NSPLIT * SLOT, 2 * NSPLIT * SLOT
        o_b = o_raw + NRAW * SLOT
        B_SIZE = 36864
        o_c = o_b + B_SIZE
        C_SIZE = arena_size - o_c
        weights = region(0, o_b)
        w_hi = weights("w_hi", [P, NSPLIT * EW], F32R)
        w_lo = weights("w_lo", [P, NSPLIT * EW], F32R)
        w_raw = weights("w_raw", [P, NRAW * EW], F32)

        r_hi0 = region(o_hi, SLOT)
        oh_m = r_hi0("oh_m", [P, NSEL, P], F32)
        r_hi12 = region(o_hi + SLOT, 2 * SLOT)
        x_raw = r_hi12("x_raw", [P, NBATCH, KH, SEQ], F32)
        wsum = [r_hi12("wsum0", [P, H], F32)]
        r_lo0 = region(o_lo, SLOT)
        oh_q = r_lo0("oh_q", [P, NSEL, 2, TQ], F32)
        g_sb = r_lo0("g_sb", [P, KH, RR], F32)
        mqg = r_lo0("mqg", [RR, NBATCH, NEXP], F32)
        tok_f, emp_f = [r_lo0(n, [P, TQ], F32) for n in ("tok_f", "emp_f")]
        r_lo12 = region(o_lo + SLOT, 2 * SLOT)
        x_hi = [r_lo12(f"x_hi{i}", [P, KH, SEQ], F32R) for i in range(2)]
        x_lo = [r_lo12(f"x_lo{i}", [P, KH, SEQ], F32R) for i in range(2)]
        wsum.append(r_lo12("wsum1", [P, H], F32))
        r_raw0 = region(o_raw, SLOT)
        rc = r_raw0("rc", [P, RW], F32)
        tri = r_raw0("tri", [P, P], BF16)
        ones = r_raw0("ones", [P, P], BF16)
        rt = [r_raw0(f"rt{i}", [P, CH, NEXP], F32) for i in range(7)]
        chosen = r_raw0("chosen", [P, CH, NEXP], BF16)
        cc = [r_raw0(f"cc{i}", [P, CH], F32) for i in range(12)]
        slot_f, place_f, tile_f = [r_raw0(n, [P, NSEL], F32) for n in ("slot_f", "place_f", "tile_f")]
        slot_i, part_i = [r_raw0(n, [P, NSEL], I32) for n in ("slot_i", "part_i")]
        trows = [r_raw0(f"trow{i}", [1, 1, TQ], F32) for i in range(3)]
        run_i = r_raw0("run_i", [1, TQ], I32)
        t_row = r_raw0("t_row", [P, TQ, NEXP], F32)
        r_raw1 = region(o_raw + SLOT, SLOT)
        wt_sb = r_raw1("wt_sb", [P, KH, H], F32)
        wpt_sb = r_raw1("wpt_sb", [P, KH, H], F32)

        r_b = region(o_b, B_SIZE)
        wbt_sb = r_b("wbt_sb", [P, KH, H], F32)
        wb_sb = r_b("wb_sb", [P, KH, H], F32)
        mqt = r_b("mqt", [RR, NBATCH, H], F32)
        p_sb = r_b("p_sb", [RR, H], F32)
        qt_sb = r_b("qt_sb", [RR, H], F32)
        small_sb = r_b("small_sb", [P, KH, 3 * RR], F32)
        q_sb = r_b("q_sb", [P, KH, RR], F32)
        y_st = [r_b(f"y_st{i}", [P, H], F32) for i in range(2)]

        r_e = region(o_b, B_SIZE)
        xg = [r_e(f"xg{i}", [P, H], F32) for i in range(NXG)]
        xt_hi = [r_e(f"xt_hi{i}", [P, H], F32R) for i in range(2)]
        xt_lo = [r_e(f"xt_lo{i}", [P, H], F32R) for i in range(2)]
        sg = [r_e(f"sg{i}", [P, INTER], F32) for i in range(2)]
        hh = [r_e(f"hh{i}", [P, INTER], F32) for i in range(2)]
        ht_hi = [r_e(f"ht_hi{i}", [P, KI * P], F32R) for i in range(2)]
        ht_lo = [r_e(f"ht_lo{i}", [P, KI * P], F32R) for i in range(2)]
        ys = [r_e(f"ys{i}", [P, H], F32) for i in range(NYS)]

        r_c = region(o_c, C_SIZE)
        we_hi = [r_c(f"we_hi{i}", [P, KH, H], F32R) for i in range(2)]
        we_lo = [r_c(f"we_lo{i}", [P, KH, H], F32R) for i in range(2)]
        cs = r_c("cs", [P, CW], F32)
        wtab = r_c("wtab", [P, TQ], F32)
        gidx = r_c("gidx", [P, TQ], U32)
        sidx = r_c("sidx", [P, TQ], U32)
        tabs = r_c("tabs", [1, 5, TQ], I32)
        mask = r_c("mask", [RR, NBATCH], F32)
        adp_sb = r_c("adp_sb", [RR, NBATCH], I32)
        scl_sb = r_c("scl_sb", [RR, 1], F32)
        T_EXP, T_RAW, T_SPL, T_NEW, T_CNT = range(5)

        ident = cs[:, C_ID:C_ID + P]
        at_s = small_sb[:, :, 0:RR]
        bw_s = small_sb[:, :, RR:2 * RR]
        gt_s = small_sb[:, :, 2 * RR:3 * RR]

        bank = [ctx.enter_context(nc.psum_tensor(f"bank{i}", [P, 512], F32)) for i in range(8)]
        y_dram = nc.dram_tensor("y_rows", [NTOK, H], F32, kind="Internal").ap()

        d_cst, d_rc, d_small, d_wt, d_wpt, d_wb, d_wbt, d_adp, d_scl = [
            sem("d_" + n) for n in ("cst", "rc", "small", "wt", "wpt", "wb", "wbt", "adp", "scl")]
        d_x = [sem(f"d_x{b}") for b in range(NBATCH)]
        d_out = sem("d_out")
        d_y = [sem(f"d_y{i}") for i in range(2)]
        m_p, m_qt, m_q, m_qg, m_g, m_lg, m_rk, m_tb = [
            sem("m_" + n) for n in ("p", "qt", "q", "qg", "g", "lg", "rk", "tb")]
        m_we = sem("m_we")
        m_y = sem("m_y")
        a_p, a_qt, a_exp = sem("a_p"), sem("a_qt"), sem("a_exp")
        a_xhi, p_xlo = sem("a_xhi"), sem("p_xlo")
        v_ws, a_whi, p_wlo = sem("v_ws"), sem("a_whi"), sem("p_wlo")
        a_y = sem("a_y")
        v_mask, v_mqt, v_q, v_mqg, v_g = [sem("v_" + n) for n in ("mask", "mqt", "q", "mqg", "g")]
        v_sh, v_cho, v_ohm, v_q1, v_tab, v_idx, v_w = [
            sem("v_" + n) for n in ("sh", "cho", "ohm", "q1", "tab", "idx", "w")]
        v_zero = sem("v_zero")
        p_ohq = sem("p_ohq")
        v_chain, p_chain = sem("v_chain"), sem("p_chain")
        d_w = [sem(f"d_w{i}") for i in range(2)]
        d_g = [sem(f"d_g{i}") for i in range(NXG)]
        d_s = sem("d_s")
        a_gu, a_dn, v_gu, v_dn = sem("a_gu"), sem("a_dn"), sem("v_gu"), sem("v_dn")
        m_xt, m_gu, m_ht, m_dn = sem("m_xt"), sem("m_gu"), sem("m_ht"), sem("m_dn")
        a_xt, v_xt, a_sg, v_h, a_ht, v_ht, a_ys = [
            sem(n) for n in ("a_xt", "v_xt", "a_sg", "v_h", "a_ht", "v_ht", "a_ys")]

        blk = ctx.enter_context(nc.Block())

        @contextmanager
        def in_use(eng, count, t):
            if t < NFULL:
                yield
            else:
                with eng.If(count > t):
                    yield

        def tile_value(eng, row, t, hi):
            return eng.value_load(tabs[0:1, row, t:t + 1], min_val=0, max_val=hi)

        def tile_count(eng):
            eng.wait_ge(v_tab, 1)
            return tile_value(eng, T_CNT, 0, NTILE)

        def load_weights(e, count, t):
            with in_use(e, count, t):
                if t >= NRAW:
                    e.wait_ge(v_dn, t - 1)
                new = tile_value(e, T_NEW, t, 1)
                with e.If(new > 0):
                    ex = tile_value(e, T_EXP, t, NEXP - 1)
                    ring = tile_value(e, T_RAW, t, NRAW - 1)
                    e.dma_start(w_raw[:, bass.ds(ring * EW, EW)],
                                wall[bass.ds(ex, 1)].rearrange("a p n -> p (a n)")).then_inc(d_w[t % 2], 16)
                with e.Else():
                    if t >= 2:
                        e.wait_ge(d_w[t % 2], 16 * (t // 2))
                    e.sem_inc(d_w[t % 2], 16)

        def split_step(e, count, t, part, own):
            gu = part == "gu"
            off, n = (0, GUW) if gu else (GUW, DW)
            with in_use(e, count, t):
                new = tile_value(e, T_NEW, t, 1)
                with e.If(new > 0):
                    src = tile_value(e, T_RAW, t, NRAW - 1)
                    dst = tile_value(e, T_SPL, t, NSPLIT - 1)
                    s_at, d_at = e.snap(src * EW), e.snap(dst * EW)
                    act = own is a_gu or own is a_dn
                    if act:
                        e.wait_ge(d_w[t % 2], 16 * (t // 2 + 1))
                        if t == 0:
                            e.wait_ge(m_tb, 1)
                        elif t < NSPLIT:
                            e.wait_ge(m_y, CH)
                        else:
                            e.wait_ge(m_gu if gu else m_dn, t - 2)
                    else:
                        e.wait_ge(a_gu if gu else a_dn, t + 1)
                    raw = w_raw[:, bass.ds(s_at + off, n)]
                    hi = w_hi[:, bass.ds(d_at + off, n)]
                    if act:
                        e.activation(hi, raw, ACT.Copy).then_inc(own, 1)
                    else:
                        e.tensor_tensor(w_lo[:, bass.ds(d_at + off, n)], raw, hi, ALU.subtract).then_inc(own, 1)
                with e.Else():
                    if t >= 1:
                        e.wait_ge(own, t)
                    e.sem_inc(own, 1)

        @blk.sync
        def _(e):
            def load(dst, src, s):
                e.dma_start(dst, src).then_inc(s, 16)
            load(small_sb[:], small, d_small)
            load(wt_sb[:], wt, d_wt)
            load(wpt_sb[:], wpt, d_wpt)
            load(scl_sb[:], scl, d_scl)
            load(adp_sb[:], adp, d_adp)
            load(cs[:], cst, d_cst)
            load(wb_sb[:], wb, d_wb)
            load(x_raw[:, 0], xt[0], d_x[0])
            load(wbt_sb[:], wbt, d_wbt)
            for b in range(1, NBATCH):
                load(x_raw[:, b], xt[b], d_x[b])
            load(rc[:], rcst, d_rc)
            for c in range(CH):
                if c == 2:
                    e.dma_start(out, x).then_inc(d_out, 16)
                e.wait_ge(a_y, c + 1)
                e.dma_start(y_dram[c * P:(c + 1) * P, :], y_st[c % 2][:]).then_inc(d_y[c % 2], 16)
                if c == CPB * 2:
                    count = tile_count(e)
                    e.wait_ge(v_ohm, 1)
                    e.wait_ge(p_ohq, 1)
                    load_weights(e, count, 0)
                if c == CPB * 2 + 1:
                    load_weights(e, count, 1)
            for t in range(2, NTILE):
                load_weights(e, count, t)

        @blk.tensor
        def _(e):
            def k_sum(dst, pairs, first=True, last=True):
                for i, (a, b) in enumerate(pairs):
                    mm = e.matmul(dst, a, b, start=first and i == 0, stop=last and i == len(pairs) - 1)
                return mm

            e.wait_ge(d_small, 16)
            e.wait_ge(d_wt, 16)
            k_sum(bank[0][0:RR, :], [(at_s[:, k], wt_sb[:, k]) for k in range(KH)]).then_inc(m_p, 1)
            e.wait_ge(d_wpt, 16)
            k_sum(bank[1][0:RR, :], [(bw_s[:, k], wpt_sb[:, k]) for k in range(KH)]).then_inc(m_qt, 1)
            e.wait_ge(d_cst, 16)
            e.wait_ge(a_qt, 1)
            for k in range(KH):
                mm = e.transpose(bank[2][:, k * RR:(k + 1) * RR], qt_sb[:, k * P:(k + 1) * P], ident[0:RR, 0:RR])
            mm.then_inc(m_q, 1)
            e.wait_ge(v_q, 1)
            k_sum(bank[3][0:RR, 0:NEXP], [(q_sb[:, k], gt_s[:, k, 0:NEXP]) for k in range(KH)]).then_inc(m_qg, 1)
            e.wait_ge(d_wb, 16)
            e.wait_ge(a_p, 1)
            e.wait_ge(v_mqg, 1)
            for i in range(KH):
                mm = k_sum(bank[4][:, i * RR:(i + 1) * RR],
                           [(wb_sb[:, k, i * P:(i + 1) * P], gt_s[:, k]) for k in range(KH)]
                           + [(p_sb[:, i * P:(i + 1) * P], mqg[:].rearrange("p b n -> p (b n)"))])
            mm.then_inc(m_g, 1)

            def w_eff(b):
                for i in range(KH):
                    n = b * KH + i
                    if n == 0:
                        e.wait_ge(v_mqt, NBATCH)
                    if n >= 2:
                        e.wait_ge(v_ws, n - 1)
                    e.matmul(bank[n % 2][:], p_sb[:, i * P:(i + 1) * P], mqt[:, b],
                             start=True, stop=True).then_inc(m_we, 1)

            w_eff(0)
            e.wait_ge(v_g, 1)
            for c in range(CH):
                b, r = divmod(c, CPB)
                if r == 0:
                    e.wait_ge(d_x[b], 16)
                mm = k_sum(bank[6][:, c * NEXP:(c + 1) * NEXP],
                           [(x_raw[:, b, k, r * P:(r + 1) * P], g_sb[:, k, b * NEXP:(b + 1) * NEXP]) for k in range(KH)])
            mm.then_inc(m_lg, 1)

            def y_chunk(c):
                b, r = divmod(c, CPB)
                if r == 0:
                    e.wait_ge(p_xlo, b + 1)
                    e.wait_ge(p_wlo, KH * (b + 1))
                if c >= 2:
                    e.wait_ge(a_y, c - 1)
                for k in range(KH):
                    hi, lo = (v[b % 2][:, k, r * P:(r + 1) * P] for v in (x_hi, x_lo))
                    whi, wlo = we_hi[b % 2][:, k], we_lo[b % 2][:, k]
                    dst = bank[2 + c % 2][:]
                    e.matmul(dst, hi, whi, start=k == 0, stop=False)
                    e.matmul(dst, hi, wlo, start=False, stop=False)
                    mm = e.matmul(dst, lo, whi, start=False, stop=k == KH - 1)
                mm.then_inc(m_y, 1)

            def ranks():
                e.wait_ge(v_cho, 1)
                flat = chosen[:].rearrange("p c n -> p (c n)")
                W = CH * NEXP
                e.matmul(bank[5][:, 0:W], tri[:], flat, start=True, stop=True)
                for s in range(1, CH):
                    e.matmul(bank[5][:, s * NEXP:W], ones[:], flat[:, 0:W - s * NEXP],
                             start=False, stop=True, skip_group_check=True)
                for c in range(CH):
                    mm = e.matmul(bank[7][:, 0:NEXP], ones[:], chosen[:, c], start=c == 0, stop=c == CH - 1)
                mm.then_inc(m_rk, 1)

            def slot_tables():
                e.wait_ge(v_ohm, 1)
                e.wait_ge(p_ohq, 1)
                for j in range(NSEL):
                    mm = e.matmul(bank[4][:, 0:2 * TQ], oh_m[:, j], oh_q[:, j].rearrange("p a n -> p (a n)"),
                                  start=j == 0, stop=j == NSEL - 1)
                mm.then_inc(m_tb, 1)

            for c in range(CH):
                y_chunk(c)
                if c == 1:
                    ranks()
                    w_eff(1)
                if c == 6:
                    slot_tables()
                    w_eff(2)
                if c == 10:
                    w_eff(3)

            count = tile_count(e)

            def x_turn(t):
                with in_use(e, count, t):
                    e.wait_ge(d_g[t % NXG], 16 * (t // NXG + 1))
                    if t >= 1:
                        e.wait_ge(v_xt, t)
                    for k in range(KH):
                        mm = e.transpose(bank[0][:, k * P:(k + 1) * P], xg[t % NXG][:, k * P:(k + 1) * P], ident)
                    mm.then_inc(m_xt, 1)

            def h_turn(t):
                with in_use(e, count, t):
                    if t == 0:
                        e.wait_ge(v_zero, 1)
                    e.wait_ge(v_h, t + 1)
                    if t >= 1:
                        e.wait_ge(v_ht, t)
                    for k in range(KI):
                        w = P if k < KI - 1 else ILAST
                        mm = e.transpose(bank[1][0:w, k * P:(k + 1) * P], hh[t % 2][:, k * P:k * P + w], ident)
                    mm.then_inc(m_ht, 1)

            def gate_up(t):
                with in_use(e, count, t):
                    ring = tile_value(e, T_SPL, t, NSPLIT - 1)
                    at = e.snap(ring * EW)
                    e.wait_ge(v_xt, t + 1)
                    e.wait_ge(v_gu, t + 1)
                    if t >= 2:
                        e.wait_ge(v_h, t - 1)
                    for k in range(KH):
                        hi, lo = (v[t % 2][:, k * P:(k + 1) * P] for v in (xt_hi, xt_lo))
                        for a, w, last in ((hi, w_hi, False), (hi, w_lo, False), (lo, w_hi, True)):
                            for s in range(2):
                                mm = e.matmul(bank[2 + 2 * s + t % 2][:, 0:INTER], a,
                                              w[:, bass.ds(at + (k * GU + s * INTER), INTER)],
                                              start=k == 0 and a is hi and w is w_hi,
                                              stop=k == KH - 1 and last)
                    mm.then_inc(m_gu, 1)

            def down(t):
                with in_use(e, count, t):
                    ring = tile_value(e, T_SPL, t, NSPLIT - 1)
                    at = e.snap(ring * EW)
                    e.wait_ge(v_ht, t + 1)
                    e.wait_ge(v_dn, t + 1)
                    if t >= 2:
                        e.wait_ge(a_ys, t - 1)
                    for k in range(KI):
                        n = P if k < KI - 1 else ILAST
                        hi, lo = (v[t % 2][0:n, k * P:(k + 1) * P] for v in (ht_hi, ht_lo))
                        for a, w, last in ((hi, w_hi, False), (hi, w_lo, False), (lo, w_hi, True)):
                            mm = e.matmul(bank[6 + t % 2][:], a, w[0:n, bass.ds(at + (GUW + k * H), H)],
                                          start=k == 0 and a is hi and w is w_hi, stop=k == KI - 1 and last)
                    mm.then_inc(m_dn, 1)

            x_turn(0)
            for t in range(NTILE + 1):
                if t >= 1:
                    h_turn(t - 1)
                if t + 1 < NTILE:
                    x_turn(t + 1)
                if t < NTILE:
                    gate_up(t)
                if t >= 1:
                    down(t - 1)

        @blk.scalar
        def _(e):
            e.wait_ge(m_p, 1)
            e.activation(p_sb[:], bank[0][0:RR, :], ACT.Copy).then_inc(a_p, 1)
            e.wait_ge(m_qt, 1)
            e.activation(qt_sb[:], bank[1][0:RR, :], ACT.Copy).then_inc(a_qt, 1)

            def x_split(b):
                e.wait_ge(d_x[b], 16)
                if b >= 2:
                    e.wait_ge(m_y, CPB * (b - 1))
                e.activation(x_hi[b % 2][:], x_raw[:, b], ACT.Copy).then_inc(a_xhi, 1)

            def w_split(b):
                for i in range(KH):
                    n = b * KH + i
                    e.wait_ge(v_ws, n + 1)
                    if b >= 2 and i == 0:
                        e.wait_ge(m_y, CPB * (b - 1))
                    e.activation(we_hi[b % 2][:, i], wsum[n % 2][:], ACT.Copy).then_inc(a_whi, 1)

            def y_stage(c):
                e.wait_ge(m_y, c + 1)
                if c >= 2:
                    e.wait_ge(d_y[c % 2], 16 * (c // 2))
                e.activation(y_st[c % 2][:], bank[2 + c % 2][:], ACT.Copy).then_inc(a_y, 1)

            x_split(0)
            w_split(0)
            x_split(1)
            e.wait_ge(v_sh, 1)
            e.activation(rt[1][:], rt[0][:], ACT.Exp).then_inc(a_exp, 1)
            for c in range(CH):
                y_stage(c)
                if c == 1:
                    w_split(1)
                if c == 4:
                    x_split(2)
                if c == 5:
                    w_split(2)
                if c == 8:
                    x_split(3)
                if c == 9:
                    w_split(3)
            count = tile_count(e)
            split_step(e, count, 0, "gu", a_gu)
            split_step(e, count, 0, "dn", a_dn)

            def x_evac(t):
                with in_use(e, count, t):
                    e.wait_ge(m_xt, t + 1)
                    if t >= 2:
                        e.wait_ge(m_gu, t - 1)
                    e.activation(xt_hi[t % 2][:], bank[0][:], ACT.Copy).then_inc(a_xt, 1)

            def h_evac(t):
                with in_use(e, count, t):
                    e.wait_ge(m_ht, t + 1)
                    if t >= 2:
                        e.wait_ge(m_dn, t - 1)
                    e.activation(ht_hi[t % 2][:], bank[1][:, 0:KI * P], ACT.Copy).then_inc(a_ht, 1)

            def silu(t):
                with in_use(e, count, t):
                    e.wait_ge(m_gu, t + 1)
                    if t >= 2:
                        e.wait_ge(v_h, t - 1)
                    e.activation(sg[t % 2][:], bank[2 + t % 2][:, 0:INTER], ACT.Silu).then_inc(a_sg, 1)

            def y_weighted(t):
                with in_use(e, count, t):
                    if t == 0:
                        e.wait_ge(v_w, 1)
                    e.wait_ge(m_dn, t + 1)
                    if t >= NYS:
                        e.wait_ge(d_s, 16 * (t - NYS + 1))
                    e.activation(ys[t % NYS][:], bank[6 + t % 2][:], ACT.Copy, scale=wtab[:, t:t + 1]).then_inc(a_ys, 1)

            x_evac(0)
            split_step(e, count, 1, "gu", a_gu)
            split_step(e, count, 1, "dn", a_dn)
            for t in range(NTILE + 1):
                if t >= 1:
                    h_evac(t - 1)
                if t + 1 < NTILE:
                    x_evac(t + 1)
                if t + 2 < NTILE:
                    split_step(e, count, t + 2, "gu", a_gu)
                if t < NTILE:
                    silu(t)
                if t >= 1:
                    y_weighted(t - 1)
                if t + 2 < NTILE:
                    split_step(e, count, t + 2, "dn", a_dn)

        @blk.vector
        def _(e):
            done = [0]

            def step(ins):
                done[0] += 1
                ins.then_inc(v_chain, 1)
                e.wait_ge(v_chain, done[0])

            def over_e(v):
                return v.unsqueeze(2).to_broadcast([P, CH, NEXP])

            def over_c(v):
                return v.unsqueeze(1).to_broadcast([P, CH, NEXP])

            e.wait_ge(d_cst, 16)
            e.wait_ge(d_adp, 16)
            e.wait_ge(d_scl, 16)
            step(e.tensor_copy(mask[:], adp_sb[:]))
            e.tensor_scalar(mask[:], mask[:], cs[0:RR, C_ADP:C_ADP + 1], scl_sb[:, 0:1], ALU.is_equal, ALU.mult).then_inc(v_mask, 1)
            e.wait_ge(v_mask, 1)
            e.wait_ge(m_q, 1)
            e.tensor_copy(q_sb[:].rearrange("p k r -> p (k r)"), bank[2][:, 0:KH * RR]).then_inc(v_q, 1)
            for b in range(NBATCH):
                if b == 0:
                    e.wait_ge(a_qt, 1)
                e.tensor_scalar(mqt[:, b], qt_sb[:], mask[:, b:b + 1], None, ALU.mult).then_inc(v_mqt, 1)
            e.wait_ge(m_qg, 1)
            for b in range(NBATCH):
                ins = e.tensor_scalar(mqg[:, b], bank[3][0:RR, 0:NEXP], mask[:, b:b + 1], None, ALU.mult)
            ins.then_inc(v_mqg, 1)
            e.wait_ge(m_g, 1)
            e.tensor_copy(g_sb[:].rearrange("p k r -> p (k r)"), bank[4][:, 0:KH * RR]).then_inc(v_g, 1)

            def w_sum(b):
                for i in range(KH):
                    n = b * KH + i
                    if n == 0:
                        e.wait_ge(d_wbt, 16)
                    e.wait_ge(m_we, n + 1)
                    if n >= 2:
                        e.wait_ge(p_wlo, n - 1)
                    e.tensor_tensor(wsum[n % 2][:], bank[n % 2][:], wbt_sb[:, i], ALU.add).then_inc(v_ws, 1)

            w_sum(0)
            e.wait_ge(d_rc, 16)
            e.tensor_copy(tri[:], rc[:, R_TRI:R_TRI + P]).then_inc(v_chain, 1)
            e.tensor_copy(ones[:], rc[:, R_ONE:R_ONE + P]).then_inc(v_chain, 1)
            done[0] += 2

            sh, ex, t1, oh1, oh2, sh2, rank = rt
            mx, r1, m2, r2, sm, e1, e2, den, w1, w2, cA, cB = cc
            rev = over_c(rc[:, R_REV:R_REV + NEXP])
            e.wait_ge(m_lg, 1)
            lg = bank[6][:, 0:CH * NEXP].rearrange("p (c n) -> p c n", n=NEXP)
            step(e.tensor_reduce(mx[:], lg, AX_X, ALU.max))
            e.tensor_tensor(sh[:], lg, over_e(mx[:]), ALU.subtract).then_inc(v_sh, 1)
            e.wait_ge(v_sh, 1)
            step(e.scalar_tensor_tensor(t1[:], sh[:], 0.0, rev, ALU.is_ge, ALU.mult))
            step(e.tensor_reduce(r1[:], t1[:], AX_X, ALU.max))
            step(e.tensor_tensor(oh1[:], rev, over_e(r1[:]), ALU.is_equal))
            step(e.scalar_tensor_tensor(sh2[:], oh1[:], -3.0e38, sh[:], ALU.mult, ALU.add))
            step(e.tensor_reduce(m2[:], sh2[:], AX_X, ALU.max))
            step(e.tensor_tensor(t1[:], sh2[:], over_e(m2[:]), ALU.is_equal))
            step(e.tensor_tensor(t1[:], t1[:], rev, ALU.mult))
            step(e.tensor_reduce(r2[:], t1[:], AX_X, ALU.max))
            step(e.tensor_tensor(oh2[:], rev, over_e(r2[:]), ALU.is_equal))
            e.tensor_tensor(chosen[:], oh1[:], oh2[:], ALU.add).then_inc(v_cho, 1)
            e.wait_ge(a_exp, 1)
            step(e.tensor_reduce(sm[:], ex[:], AX_X, ALU.add))
            step(e.tensor_tensor(t1[:], ex[:], oh1[:], ALU.mult))
            step(e.tensor_reduce(e1[:], t1[:], AX_X, ALU.add))
            step(e.tensor_tensor(t1[:], ex[:], oh2[:], ALU.mult))
            step(e.tensor_reduce(e2[:], t1[:], AX_X, ALU.add))
            step(e.reciprocal(cA[:], sm[:]))
            step(e.tensor_tensor(e1[:], e1[:], cA[:], ALU.mult))
            step(e.tensor_tensor(e2[:], e2[:], cA[:], ALU.mult))
            step(e.scalar_tensor_tensor(den[:], e1[:], 1e-20, e2[:], ALU.add, ALU.add))
            step(e.reciprocal(cB[:], den[:]))
            step(e.tensor_tensor(w1[:], e1[:], cB[:], ALU.mult))
            step(e.tensor_tensor(w2[:], e2[:], cB[:], ALU.mult))

            w_sum(1)

            e.wait_ge(m_rk, 1)
            cnt, ntile, end, off = (v[:, 0:NEXP] for v in (sm, e1, e2, den))
            step(e.tensor_copy(cnt, bank[7][:, 0:NEXP]))
            thr = rc[:, R_THR:R_THR + 16].unsqueeze(1).to_broadcast([P, NEXP, 16])
            step(e.tensor_tensor(t1[:], cnt.unsqueeze(2).to_broadcast([P, NEXP, 16]), thr, ALU.is_gt))
            step(e.tensor_reduce(ntile, t1[:], AX_X, ALU.add))
            cum = rc[:, R_CUM:R_CUM + 256].rearrange("p (a n) -> p a n", n=NEXP)
            step(e.tensor_tensor(t1[:], ntile.unsqueeze(1).to_broadcast([P, NEXP, NEXP]), cum, ALU.mult))
            step(e.tensor_reduce(end, t1[:], AX_X, ALU.add))
            step(e.tensor_tensor(off, end, ntile, ALU.subtract))
            step(e.tensor_scalar(off, off, float(P), None, ALU.mult))
            rk = bank[5][:, 0:CH * NEXP].rearrange("p (c n) -> p c n", n=NEXP)
            step(e.tensor_tensor(rank[:], rk, over_c(off), ALU.add))
            slot = slot_f[:]
            for k, oh in enumerate((oh1, oh2)):
                step(e.tensor_tensor(t1[:], oh[:], rank[:], ALU.mult))
                step(e.tensor_reduce(slot[:, k * CH:(k + 1) * CH], t1[:], AX_X, ALU.add))
            step(e.tensor_copy(slot_i[:], slot))
            step(e.tensor_single_scalar(part_i[:], slot_i[:], P - 1, ALU.bitwise_and))
            step(e.tensor_copy(place_f[:], part_i[:]))
            step(e.tensor_single_scalar(part_i[:], slot_i[:], 7, ALU.arith_shift_right))
            step(e.tensor_copy(tile_f[:], part_i[:]))
            iqs = cs[:, C_IQ:C_IQ + TQ].unsqueeze(1).to_broadcast([P, NSEL, TQ])
            e.tensor_tensor(oh_q[:, :, 0], tile_f[:].unsqueeze(2).to_broadcast([P, NSEL, TQ]), iqs, ALU.is_equal).then_inc(v_q1, 1)

            iq = cs[0:1, C_IQ:C_IQ + TQ]
            end1, nt1 = end[0:1], ntile[0:1]
            tr = t_row[0:1]
            step(e.tensor_tensor(tr, iq.unsqueeze(2).to_broadcast([1, TQ, NEXP]),
                                 end1.unsqueeze(1).to_broadcast([1, TQ, NEXP]), ALU.is_ge))
            ef, rf, tf = (v[0:1] for v in trows)
            step(e.tensor_reduce(ef[:, 0], tr, AX_X, ALU.add))
            step(e.tensor_scalar(nt1, nt1, 0.0, None, ALU.is_gt))
            step(e.tensor_tensor(tr, tr, nt1.unsqueeze(1).to_broadcast([1, TQ, NEXP]), ALU.mult))
            step(e.tensor_reduce(rf[:, 0], tr, AX_X, ALU.add))
            step(e.tensor_scalar(tabs[:, T_EXP], ef[:, 0], float(NEXP - 1), None, ALU.min))
            step(e.tensor_tensor(tf[:, 0, 1:TQ], rf[:, 0, 1:TQ], rf[:, 0, 0:TQ - 1], ALU.is_gt))
            step(e.memset(tf[:, 0, 0:1], 1.0))
            step(e.tensor_copy(tabs[:, T_NEW], tf[:, 0]))
            step(e.tensor_copy(run_i[:], rf[:, 0]))
            step(e.tensor_single_scalar(tabs[:, T_RAW], run_i[:], NRAW - 1, ALU.bitwise_and))
            th3 = rc[0:1, R_TH3:R_TH3 + 5]
            t3 = t_row[0:1, :, 0:5]
            step(e.tensor_tensor(t3, rf[:, 0].unsqueeze(2).to_broadcast([1, TQ, 5]),
                                 th3.unsqueeze(1).to_broadcast([1, TQ, 5]), ALU.is_ge))
            step(e.tensor_reduce(ef[:, 0], t3, AX_X, ALU.add))
            step(e.scalar_tensor_tensor(tabs[:, T_SPL], ef[:, 0], -float(NSPLIT), rf[:, 0], ALU.mult, ALU.add))
            e.tensor_copy(tabs[:, T_CNT, 0:1], end[0:1, NEXP - 1:NEXP]).then_inc(v_tab, 1)

            im = rc[:, R_IM:R_IM + P].unsqueeze(1).to_broadcast([P, NSEL, P])
            e.tensor_tensor(oh_m[:], place_f[:].unsqueeze(2).to_broadcast([P, NSEL, P]), im, ALU.is_equal).then_inc(v_ohm, 1)
            w_sum(2)
            e.wait_ge(m_tb, 1)
            step(e.tensor_scalar(tok_f[:], bank[4][:, 0:TQ], 1.0, None, ALU.subtract))
            e.tensor_copy(wtab[:], bank[4][:, TQ:2 * TQ]).then_inc(v_w, 1)
            step(e.tensor_scalar(gidx[:], tok_f[:], 0.0, None, ALU.max))
            step(e.tensor_scalar(emp_f[:], tok_f[:], 0.0, float(SKIP), ALU.is_lt, ALU.mult))
            e.tensor_tensor(sidx[:], tok_f[:], emp_f[:], ALU.add).then_inc(v_idx, 1)
            w_sum(3)

            e.wait_ge(v_ws, NBATCH * KH)
            e.memset(bank[1][ILAST:P, (KI - 1) * P:KI * P], 0.0).then_inc(v_zero, 1)
            count = tile_count(e)
            split_step(e, count, 0, "gu", v_gu)
            split_step(e, count, 0, "dn", v_dn)

            def x_low(t):
                with in_use(e, count, t):
                    e.wait_ge(a_xt, t + 1)
                    e.tensor_tensor(xt_lo[t % 2][:], bank[0][:], xt_hi[t % 2][:], ALU.subtract).then_inc(v_xt, 1)

            def h_low(t):
                with in_use(e, count, t):
                    e.wait_ge(a_ht, t + 1)
                    e.tensor_tensor(ht_lo[t % 2][:], bank[1][:, 0:KI * P], ht_hi[t % 2][:], ALU.subtract).then_inc(v_ht, 1)

            def product(t):
                with in_use(e, count, t):
                    e.wait_ge(a_sg, t + 1)
                    if t >= 2:
                        e.wait_ge(m_ht, t - 1)
                    e.tensor_tensor(hh[t % 2][:], sg[t % 2][:], bank[4 + t % 2][:, 0:INTER], ALU.mult).then_inc(v_h, 1)

            x_low(0)
            split_step(e, count, 1, "gu", v_gu)
            split_step(e, count, 1, "dn", v_dn)
            for t in range(NTILE + 1):
                if t >= 1:
                    h_low(t - 1)
                if t + 1 < NTILE:
                    x_low(t + 1)
                if t + 2 < NTILE:
                    split_step(e, count, t + 2, "gu", v_gu)
                if t < NTILE:
                    product(t)
                if t + 2 < NTILE:
                    split_step(e, count, t + 2, "dn", v_dn)

        @blk.gpsimd
        def _(e):
            def x_low(b):
                e.wait_ge(a_xhi, b + 1)
                e.tensor_tensor(x_lo[b % 2][:], x_raw[:, b], x_hi[b % 2][:], ALU.subtract).then_inc(p_xlo, 1)

            def w_low(b):
                for i in range(KH):
                    n = b * KH + i
                    e.wait_ge(a_whi, n + 1)
                    e.tensor_tensor(we_lo[b % 2][:, i], wsum[n % 2][:], we_hi[b % 2][:, i], ALU.subtract).then_inc(p_wlo, 1)

            x_low(0)
            w_low(0)
            x_low(1)
            w_low(1)
            e.wait_ge(v_q1, 1)
            for k, w in enumerate((cc[8], cc[9])):
                e.tensor_tensor(oh_q[:, k * CH:(k + 1) * CH, 1], oh_q[:, k * CH:(k + 1) * CH, 0],
                                w[:].unsqueeze(2).to_broadcast([P, CH, TQ]), ALU.mult).then_inc(p_chain, 1)
            e.wait_ge(p_chain, TOPK)
            tok = cs[:, C_TOK:C_TOK + CH].unsqueeze(2).to_broadcast([P, CH, TQ])
            for k in range(TOPK):
                ins = e.tensor_tensor(oh_q[:, k * CH:(k + 1) * CH, 0], oh_q[:, k * CH:(k + 1) * CH, 0], tok, ALU.mult)
            ins.then_inc(p_ohq, 1)
            for b in (2, 3):
                x_low(b)
                w_low(b)

            count = tile_count(e)
            e.wait_ge(v_idx, 1)
            for i in range(2):
                e.wait_ge(d_y[i], 16 * (CH // 2))
            e.wait_ge(d_out, 16)

            def gather(t):
                with in_use(e, count, t):
                    if t >= NXG:
                        e.wait_ge(m_xt, t - NXG + 1)
                    e.indirect_dma_start(out=xg[t % NXG][:], out_offset=None, in_=y_dram,
                                         in_offset=bass.IndirectOffsetOnAxis(ap=gidx[:, t:t + 1], axis=0)
                                         ).then_inc(d_g[t % NXG], 16)

            def scatter(t):
                with in_use(e, count, t):
                    e.wait_ge(a_ys, t + 1)
                    if t >= 1:
                        e.wait_ge(d_s, 16 * t)
                    e.indirect_dma_start(out=out, out_offset=bass.IndirectOffsetOnAxis(ap=sidx[:, t:t + 1], axis=0),
                                         in_=ys[t % NYS][:], in_offset=None, bounds_check=NTOK - 1,
                                         oob_is_err=False, compute_op=ALU.add).then_inc(d_s, 16)
                    if t >= NFULL - 1:
                        e.wait_ge(d_s, 16 * (t + 1))

            for t in range(NXG - 1):
                gather(t)
            for t in range(NTILE):
                if t + NXG - 1 < NTILE:
                    gather(t + NXG - 1)
                scatter(t)


def kernel(**inputs):
    import numpy as np
    import concourse.bacc as bacc
    from concourse.bass_utils import run_bass_kernel_spmd

    get = {k: np.asarray(v) for k, v in inputs.items()}

    def chunks(a):
        return a.reshape(KH, P, -1).transpose(1, 0, 2)

    cst = np.zeros((P, CW), np.float32)
    cst[:, C_ID:C_ID + P] = np.eye(P)
    cst[:, C_IQ:C_IQ + TQ] = np.arange(TQ)
    cst[:, C_TOK:C_TOK + CH] = np.arange(CH) * P + np.arange(P)[:, None] + 1
    cst[:, C_ADP] = np.arange(P) // RANK
    rcst = np.zeros((P, RW), np.float32)
    rcst[:, R_TRI:R_TRI + P] = np.triu(np.ones((P, P)), 1)
    rcst[:, R_ONE:R_ONE + P] = 1
    rcst[:, R_REV:R_REV + NEXP] = NEXP - np.arange(NEXP)
    rcst[:, R_THR:R_THR + 16] = P * np.arange(16)
    rcst[:, R_CUM:R_CUM + 256] = np.tril(np.ones((NEXP, NEXP))).reshape(-1)
    rcst[:, R_IM:R_IM + P] = np.arange(P)
    rcst[:, R_TH3:R_TH3 + 5] = NSPLIT * np.arange(1, 6)

    x = get["x"]
    xt = x.reshape(NBATCH, SEQ, KH, P).transpose(0, 3, 2, 1)
    at = chunks(get["L0_cond_A"].reshape(RR, H).T)
    bw = chunks(get["L0_cond_B_w"].transpose(1, 0, 2).reshape(H, RR))
    gt = chunks(np.concatenate([get["L0_ffn_gate_w"].T] * NBATCH, axis=1))
    small = np.concatenate([at, bw, gt], axis=2)
    adp = np.repeat(get["itok_B_0_3"][None, :], RR, axis=0)
    scl = np.repeat(get["L0_cond_scaling"], RANK)[:, None]
    gu = np.concatenate([get[n].transpose(0, 2, 1).reshape(NEXP, KH, P, INTER) for n in ("L0_ffn_w_gate", "L0_ffn_w_up")], axis=3)
    gu = gu.transpose(0, 2, 1, 3).reshape(NEXP, P, GUW)
    dn = np.zeros((NEXP, KI * P, H), np.float32)
    dn[:, :INTER] = get["L0_ffn_w_down"].transpose(0, 2, 1)
    dn = dn.reshape(NEXP, KI, P, H).transpose(0, 2, 1, 3).reshape(NEXP, P, DW)
    arrays = {
        "cst": cst, "rcst": rcst, "small": small, "adp": adp, "scl": scl,
        "wt": chunks(get["L0_cond_Wt"]), "wpt": chunks(get["L0_cond_Wp"].T),
        "wb": chunks(get["L0_cond_W_base"]), "wbt": chunks(get["L0_cond_W_base"].T),
        "xt": xt, "x": x.reshape(NTOK, H), "wall": np.concatenate([gu, dn], axis=2),
    }
    arrays = {k: np.ascontiguousarray(v) for k, v in arrays.items()}

    nc = bacc.Bacc("TRN2", target_bir_lowering=False, num_devices=1)
    aps = {k: nc.dram_tensor(k, v.shape, mybir.dt.from_np(v.dtype), kind="ExternalInput").ap() for k, v in arrays.items()}
    out = nc.dram_tensor("out", (NTOK, H), F32, kind="ExternalOutput").ap()
    build(nc, out=out, **aps)
    r = run_bass_kernel_spmd(nc, [arrays], core_ids=[0])
    return r.results[0]["out"].reshape(NBATCH, SEQ, H)
```

```python
from contextlib import ExitStack, contextmanager, nullcontext

import concourse.bass as bass
from concourse import mybir

P = 128
F32 = mybir.dt.float32
F32R = mybir.dt.float32r
BF16 = mybir.dt.bfloat16
I32 = mybir.dt.int32
U32 = mybir.dt.uint32
ALU = mybir.AluOpType
ACT = mybir.ActivationFunctionType
AX_X = mybir.AxisListType.X

NBATCH, SEQ, H = 4, 512, 512
NADAPT, RANK = 4, 16
NEXP, INTER, TOPK = 16, 352, 2
NTOK = NBATCH * SEQ
KH = H // P
RR = NADAPT * RANK
CH = NTOK // P
CPB = CH // NBATCH
NSEL = CH * TOPK
KI = -(-INTER // P)
ILAST = INTER - (KI - 1) * P
NTILE = (NTOK * TOPK + NEXP * (P - 1)) // P
NFULL = NTOK * TOPK // P
TQ = 48
GU = 2 * INTER
GUW = KH * GU
DW = KI * H
EW = GUW + DW
WIDE = 5 * NEXP
NRAW, NSPLIT = 2, 3
C_LOAD = 9
NXG, NYS = 4, 3
W_NEW, W_SLOT = NEXP, 2 * NEXP
SKIP = 4096

SM = 3 * P
C_ID, C_IQ, C_TOK, C_ADP, CW = 0, P, P + TQ, P + TQ + CH, P + TQ + CH + 1
R_TRI, R_ONE, R_REV, R_THR, R_CUM, R_TH3, R_IM, RW = 0, P, 2 * P, 2 * P + 16, 2 * P + 32, 2 * P + 288, 2 * P + 293, 3 * P + 293


def build(nc, cst, rcst, small, adp, scl, wt, wpt, wb, wbt, xt, x, wall, out):
    with ExitStack() as ctx:
        sem_names = []

        def sem(name):
            sem_names.append(name)
            return ctx.enter_context(nc.semaphore(name))

        arena0 = -(-nc.sbuf_base // 64) * 64
        arena_size = nc.sbuf_usable_end // 64 * 64 - arena0

        def region(start, size):
            at = [start]

            def place(name, shape, dt):
                nbytes = 2 if dt == BF16 else 4
                for s in shape[1:]:
                    nbytes *= s
                nbytes = -(-nbytes // 32) * 32
                assert at[0] + nbytes <= start + size, (name, at[0] + nbytes - start - size)
                t = nc.alloc_sbuf_tensor_at(name, shape, dt, offset=arena0 + at[0])
                at[0] += nbytes
                return t
            return place

        SLOT = EW * 4
        o_hi, o_lo, o_raw = 0, NSPLIT * SLOT, 2 * NSPLIT * SLOT
        o_b = o_raw + NRAW * SLOT
        B_SIZE = 36864
        o_c = o_b + B_SIZE
        C_SIZE = arena_size - o_c
        weights = region(0, o_b)
        w_hi = weights("w_hi", [P, NSPLIT * EW], F32R)
        w_lo = weights("w_lo", [P, NSPLIT * EW], F32R)
        w_raw = weights("w_raw", [P, NRAW * EW], F32)

        r_hi0 = region(o_hi, SLOT)
        x_st = [r_hi0(f"x_st{i}", [P, KH, SEQ], F32) for i in range(2)]
        mqg = r_hi0("mqg", [RR, 2, NBATCH, NEXP], F32)
        oh_m = region(o_hi, SLOT)("oh_m", [P, NSEL, P], F32)
        r_hi12 = region(o_hi + SLOT, 2 * SLOT)
        x_hi = r_hi12("x_hi", [P, NBATCH, KH, SEQ], F32R)
        wsum = [r_hi12("wsum0", [P, H], F32)]
        r_lo0 = region(o_lo, SLOT)
        oh_q = r_lo0("oh_q", [P, NSEL, 2, TQ], F32)
        tok_f, emp_f = [r_lo0(n, [P, TQ], F32) for n in ("tok_f", "emp_f")]
        small_sb = region(o_lo, SLOT)("small_sb", [P, KH, SM], F32)
        r_lo12 = region(o_lo + SLOT, 2 * SLOT)
        x_lo = r_lo12("x_lo", [P, NBATCH, KH, SEQ], F32R)
        wsum.append(r_lo12("wsum1", [P, H], F32))
        r_raw0 = region(o_raw, SLOT)
        rc = r_raw0("rc", [P, RW], F32)
        tri = r_raw0("tri", [P, P], BF16)
        ones = r_raw0("ones", [P, P], BF16)
        r_g = region(o_raw + 4096, SLOT - 4096)
        gt_sb = r_g("gt_sb", [P, H], F32)
        g_hi, g_lo = [r_g(n, [P, KH, P], F32R) for n in ("g_hi", "g_lo")]
        lt_sb = [r_g(f"lt_sb{i}", [NEXP, SEQ], F32) for i in range(2)]
        r_t = region(o_raw + 4096, SLOT - 4096)
        rt = [r_t(f"rt{i}", [P, CH, NEXP], F32) for i in range(7)]
        chosen = r_t("chosen", [P, CH, NEXP], BF16)
        cc = [r_t(f"cc{i}", [P, CH], F32) for i in range(12)]
        slot_f, place_f, tile_f = [r_t(n, [P, NSEL], F32) for n in ("slot_f", "place_f", "tile_f")]
        slot_i, part_i = [r_t(n, [P, NSEL], I32) for n in ("slot_i", "part_i")]
        t_row = r_t("t_row", [1, TQ, NEXP], F32)
        trows = [r_t(f"trow{i}", [1, 1, TQ], F32) for i in range(3)]
        r_raw1 = region(o_raw + SLOT, SLOT)
        wt_sb = r_raw1("wt_sb", [P, KH, H], F32)
        wpt_sb = r_raw1("wpt_sb", [P, KH, H], F32)

        r_b = region(o_b, B_SIZE)
        wbt_sb = r_b("wbt_sb", [P, KH, H], F32)
        wb_sb = r_b("wb_sb", [P, KH, H], F32)
        mq_hi = [r_b(f"mq_hi{i}", [P, H], F32R) for i in range(2)]
        mq_lo = [r_b(f"mq_lo{i}", [P, H], F32R) for i in range(2)]
        p_st = r_b("p_st", [P, H], F32R)
        p_sb = r_b("p_sb", [RR, H], F32)
        qt_sb = r_b("qt_sb", [P, H], F32)
        q_sb = r_b("q_sb", [P, KH, RR], F32)
        y_st = [r_b(f"y_st{i}", [P, H], F32) for i in range(2)]

        r_e = region(o_b, B_SIZE)
        xg = [r_e(f"xg{i}", [P, H], F32) for i in range(NXG)]
        xt_hi = [r_e(f"xt_hi{i}", [P, H], F32R) for i in range(2)]
        xt_lo = [r_e(f"xt_lo{i}", [P, H], F32R) for i in range(2)]
        sg = [r_e(f"sg{i}", [P, INTER], F32) for i in range(2)]
        hh = [r_e(f"hh{i}", [P, INTER], F32) for i in range(2)]
        ht_hi = [r_e(f"ht_hi{i}", [P, KI * P], F32R) for i in range(2)]
        ht_lo = [r_e(f"ht_lo{i}", [P, KI * P], F32R) for i in range(2)]
        ys = [r_e(f"ys{i}", [P, H], F32) for i in range(NYS)]

        r_c = region(o_c, C_SIZE)
        we_hi = [r_c(f"we_hi{i}", [P, KH, H], F32R) for i in range(2)]
        we_lo = [r_c(f"we_lo{i}", [P, KH, H], F32R) for i in range(2)]
        cs = r_c("cs", [P, CW], F32)
        wtab = r_c("wtab", [P, TQ], F32)
        gidx = r_c("gidx", [P, TQ], U32)
        sidx = r_c("sidx", [P, TQ], U32)
        T_WORD, T_CNT, T_REX, NTAB = range(4)
        tabs = r_c("tabs", [1, NTAB, TQ], I32)
        mask = r_c("mask", [P, NBATCH], F32)
        adp_sb = r_c("adp_sb", [P, NBATCH], I32)
        scl_sb = r_c("scl_sb", [P, 1], F32)

        ident = cs[:, C_ID:C_ID + P]
        at_s = small_sb[:, :, 0:P]
        bw_s = small_sb[:, :, P:2 * P]
        gt_s = small_sb[:, :, 2 * P:3 * P]

        bank = [ctx.enter_context(nc.psum_tensor(f"bank{i}", [P, 512], F32)) for i in range(8)]
        y_dram = nc.dram_tensor("y_rows", [NTOK, H], F32, kind="Internal").ap()

        d_cst, d_rc, d_small, d_wt, d_wpt, d_wb, d_wbt, d_adp, d_scl = [
            sem("d_" + n) for n in ("cst", "rc", "small", "wt", "wpt", "wb", "wbt", "adp", "scl")]
        d_x = [sem(f"d_x{b}") for b in range(NBATCH)]
        d_out = sem("d_out")
        d_y = [sem(f"d_y{i}") for i in range(2)]
        m_p, m_qt, m_q, m_qg, m_g, m_gt, m_lt, m_lg, m_rk, m_tb = [
            sem("m_" + n) for n in ("p", "qt", "q", "qg", "g", "gt", "lt", "lg", "rk", "tb")]
        m_we = sem("m_we")
        m_y = sem("m_y")
        a_p, a_qt, a_g, a_ghi, a_lt, a_exp = [sem("a_" + n) for n in ("p", "qt", "g", "ghi", "lt", "exp")]
        a_xhi, v_xlo = sem("a_xhi"), sem("v_xlo")
        v_ws, a_whi, p_wlo = sem("v_ws"), sem("a_whi"), sem("p_wlo")
        a_y = sem("a_y")
        v_mask, v_mq, v_mqlo, v_q, v_mqg, v_plo, v_glo = [
            sem("v_" + n) for n in ("mask", "mq", "mqlo", "q", "mqg", "plo", "glo")]
        v_sh, v_cho, v_ohm, v_q1, v_tab, v_idx, v_w = [
            sem("v_" + n) for n in ("sh", "cho", "ohm", "q1", "tab", "idx", "w")]
        v_zero = sem("v_zero")
        p_ohq = sem("p_ohq")
        v_chain, p_chain = sem("v_chain"), sem("p_chain")
        d_w = [sem(f"d_w{i}") for i in range(NRAW)]
        d_g = [sem(f"d_g{i}") for i in range(NXG)]
        d_s = sem("d_s")
        a_gu, a_dn, v_gu, v_dn = sem("a_gu"), sem("a_dn"), sem("v_gu"), sem("v_dn")
        m_xt, m_gu, m_ht, m_dn = sem("m_xt"), sem("m_gu"), sem("m_ht"), sem("m_dn")
        a_xt, v_xt, a_sg, v_h, a_ht, v_ht, a_ys = [
            sem(n) for n in ("a_xt", "v_xt", "a_sg", "v_h", "a_ht", "v_ht", "a_ys")]

        blk = ctx.enter_context(nc.Block())

        @contextmanager
        def in_use(eng, count, t):
            if t < NFULL:
                yield
            else:
                with eng.If(count > t):
                    yield

        def table(eng, row, at, least, most):
            return nc.values_load(tabs[0:1, row, at:at + 1], engines=[eng.engine], min_val=least, max_val=most,
                                  skip_runtime_bounds_check_because="made on the chip, from counts that the shapes bound")

        def tile_count(eng):
            eng.wait_ge(v_tab, 1)
            return table(eng, T_CNT, 0, NFULL, NTILE)

        def tile_word(eng, t):
            word = table(eng, T_WORD, t, 0, W_SLOT * NSPLIT - 1)
            run = eng.snap(word & (NEXP - 1))
            return run, eng.snap((word // W_NEW) & 1), eng.snap((run & 1) * EW), eng.snap((word // W_SLOT) * EW)

        def load_weights(e, runs, r):
            with e.If(runs > r) if r >= TOPK else nullcontext():
                if r >= NRAW:
                    e.wait_ge(v_dn, r - NRAW + 1)
                ex = table(e, T_REX, r, 0, NEXP - 1)
                e.dma_start(w_raw[:, r % NRAW * EW:(r % NRAW + 1) * EW],
                            wall[bass.ds(ex, 1)].rearrange("a p n -> p (a n)")).then_inc(d_w[r % NRAW], 16)

        def split_weights(e, count, t, word, part, own):
            gu = part == "gu"
            off, n = (0, GUW) if gu else (GUW, DW)
            act = own is a_gu or own is a_dn
            if t == 0:
                if act:
                    e.wait_ge(d_w[0], 16)
                    e.wait_ge(m_tb, 1)
                else:
                    e.wait_ge(a_gu if gu else a_dn, 1)
                split_part(e, act, off, off, n, own)
                return
            run, new, src, dst = word
            with in_use(e, count, t):
                with e.If(new > 0):
                    if act:
                        e.wait_ge(d_w[0], (run // 2 + 1) * 16)
                        e.wait_ge(d_w[1], ((run + 1) // 2) * 16)
                        if t < NSPLIT:
                            e.wait_ge(m_y, CH)
                        else:
                            e.wait_ge(m_gu if gu else m_dn, t - 2)
                    else:
                        e.wait_ge(a_gu if gu else a_dn, run + 1)
                    split_part(e, act, src + off, dst + off, n, own)

        def split_part(e, act, src, dst, n, own):
            raw, hi = w_raw[:, bass.ds(src, n)], w_hi[:, bass.ds(dst, n)]
            if act:
                e.activation(hi, raw, ACT.Copy).then_inc(own, 1)
            else:
                e.tensor_tensor(w_lo[:, bass.ds(dst, n)], raw, hi, ALU.subtract).then_inc(own, 1)

        @blk.sync
        def _(e):
            def load(dst, src, s):
                e.dma_start(dst, src).then_inc(s, 16)
            load(small_sb[:], small, d_small)
            load(wt_sb[:], wt, d_wt)
            load(wpt_sb[:], wpt, d_wpt)
            load(scl_sb[:], scl, d_scl)
            load(adp_sb[:], adp, d_adp)
            load(cs[:], cst, d_cst)
            load(wb_sb[:], wb, d_wb)
            for b in range(2):
                load(x_st[b][:], xt[b], d_x[b])
            load(wbt_sb[:], wbt, d_wbt)
            load(rc[:], rcst, d_rc)
            for b in range(2, NBATCH):
                e.wait_ge(v_xlo, b - 1)
                load(x_st[b % 2][:], xt[b], d_x[b])
            for c in range(CH):
                if c == 1:
                    e.dma_start(out, x).then_inc(d_out, 16)
                e.wait_ge(a_y, c + 1)
                e.dma_start(y_dram[c * P:(c + 1) * P, :], y_st[c % 2][:]).then_inc(d_y[c % 2], 16)
                if c == C_LOAD:
                    e.wait_ge(v_tab, 1)
                    runs = table(e, T_CNT, 1, TOPK, NEXP)
                    e.wait_ge(v_ohm, 1)
                    e.wait_ge(p_ohq, 1)
                if c in (C_LOAD, C_LOAD + 1):
                    load_weights(e, runs, c - C_LOAD)
            for r in range(2, NEXP):
                load_weights(e, runs, r)

        @blk.tensor
        def _(e):
            def k_sum(dst, pairs, first=True, last=True):
                for i, (a, b) in enumerate(pairs):
                    mm = e.matmul(dst, a, b, start=first and i == 0, stop=last and i == len(pairs) - 1)
                return mm

            e.wait_ge(d_small, 16)
            e.wait_ge(d_wt, 16)
            k_sum(bank[0][:], [(at_s[:, k], wt_sb[:, k]) for k in range(KH)]).then_inc(m_p, 1)
            e.wait_ge(d_wpt, 16)
            k_sum(bank[1][:], [(bw_s[:, k], wpt_sb[:, k]) for k in range(KH)]).then_inc(m_qt, 1)
            e.wait_ge(d_cst, 16)
            e.wait_ge(a_qt, 1)
            for k in range(KH):
                mm = e.transpose(bank[2][:, k * RR:(k + 1) * RR], qt_sb[0:RR, k * P:(k + 1) * P], ident[0:RR, 0:RR])
            mm.then_inc(m_q, 1)
            e.wait_ge(v_q, 1)
            k_sum(bank[3][0:RR, 0:NEXP], [(q_sb[:, k], gt_s[:, k, 0:NEXP]) for k in range(KH)]).then_inc(m_qg, 1)
            e.wait_ge(d_wb, 16)
            e.wait_ge(a_p, 2)
            k_sum(bank[4][:], [(gt_s[:, k], wb_sb[:, k]) for k in range(KH)], last=False)
            e.wait_ge(v_mqg, 1)
            k_sum(bank[4][:], [(mqg[:].rearrange("p a b n -> p (a b n)"), p_sb[:])], first=False).then_inc(m_g, 1)

            def w_eff(b):
                e.wait_ge(v_mqlo, b + 1)
                if b == 0:
                    e.wait_ge(v_plo, 1)
                for i in range(KH):
                    n = b * KH + i
                    if n >= 2:
                        e.wait_ge(v_ws, n - 1)
                    k_sum(bank[n % 2][:], [(p_st[:, i * P:(i + 1) * P], mq[b % 2][:]) for mq in (mq_hi, mq_lo)]
                          ).then_inc(m_we, 1)

            e.wait_ge(a_g, 1)
            for k in range(KH):
                mm = e.transpose(bank[3][:, k * P:(k + 1) * P], gt_sb[:, k * P:(k + 1) * P], ident)
            mm.then_inc(m_gt, 1)
            w_eff(0)

            def logits(b):
                if b == 0:
                    e.wait_ge(v_glo, 1)
                e.wait_ge(v_xlo, b + 1)
                if b >= 2:
                    e.wait_ge(a_lt, b - 1)
                g = slice(b * NEXP, b * NEXP + WIDE)
                k_sum(bank[6 + b % 2][0:WIDE, :],
                      [pair for k in range(KH) for pair in (
                          (g_hi[:, k, g], x_hi[:, b, k]), (g_hi[:, k, g], x_lo[:, b, k]), (g_lo[:, k, g], x_hi[:, b, k]))]
                      ).then_inc(m_lt, 1)

            def logits_turn(b):
                e.wait_ge(a_lt, b + 1)
                for r in range(CPB):
                    c = b * CPB + r
                    mm = e.transpose(bank[5][:, c * NEXP:(c + 1) * NEXP], lt_sb[b % 2][:, r * P:(r + 1) * P],
                                     ident[0:NEXP, 0:NEXP])
                mm.then_inc(m_lg, 1)

            logits(0)
            w_eff(1)
            for b in range(1, NBATCH):
                logits(b)
                logits_turn(b - 1)
            logits_turn(NBATCH - 1)

            def y_chunk(c):
                b, r = divmod(c, CPB)
                if r == 0:
                    e.wait_ge(p_wlo, KH * (b + 1))
                if c >= 2:
                    e.wait_ge(a_y, c - 1)
                for k in range(KH):
                    hi, lo = (v[:, b, k, r * P:(r + 1) * P] for v in (x_hi, x_lo))
                    whi, wlo = we_hi[b % 2][:, k], we_lo[b % 2][:, k]
                    dst = bank[2 + c % 2][:]
                    e.matmul(dst, hi, whi, start=k == 0, stop=False)
                    e.matmul(dst, hi, wlo, start=False, stop=False)
                    mm = e.matmul(dst, lo, whi, start=False, stop=k == KH - 1)
                mm.then_inc(m_y, 1)

            def ranks():
                e.wait_ge(v_cho, 1)
                flat = chosen[:].rearrange("p c n -> p (c n)")
                W = CH * NEXP
                e.matmul(bank[6][:, 0:W], tri[:], flat, start=True, stop=True)
                for s in range(1, CH):
                    e.matmul(bank[6][:, s * NEXP:W], ones[:], flat[:, 0:W - s * NEXP],
                             start=False, stop=True, skip_group_check=True)
                for c in range(CH):
                    mm = e.matmul(bank[7][:, 0:NEXP], ones[:], chosen[:, c], start=c == 0, stop=c == CH - 1)
                mm.then_inc(m_rk, 1)

            def slot_tables():
                e.wait_ge(v_ohm, 1)
                e.wait_ge(p_ohq, 1)
                for j in range(NSEL):
                    mm = e.matmul(bank[4][:, 0:2 * TQ], oh_m[:, j], oh_q[:, j].rearrange("p a n -> p (a n)"),
                                  start=j == 0, stop=j == NSEL - 1)
                mm.then_inc(m_tb, 1)

            for c in range(CH):
                y_chunk(c)
                if c == 1:
                    ranks()
                if c == 5:
                    w_eff(2)
                if c == 7:
                    slot_tables()
                if c == 9:
                    w_eff(3)

            count = tile_count(e)

            def x_turn(t):
                with in_use(e, count, t):
                    e.wait_ge(d_g[t % NXG], 16 * (t // NXG + 1))
                    if t >= 1:
                        e.wait_ge(v_xt, t)
                    for k in range(KH):
                        mm = e.transpose(bank[0][:, k * P:(k + 1) * P], xg[t % NXG][:, k * P:(k + 1) * P], ident)
                    mm.then_inc(m_xt, 1)

            def h_turn(t):
                with in_use(e, count, t):
                    if t == 0:
                        e.wait_ge(v_zero, 1)
                    e.wait_ge(v_h, t + 1)
                    if t >= 1:
                        e.wait_ge(v_ht, t)
                    for k in range(KI):
                        w = P if k < KI - 1 else ILAST
                        mm = e.transpose(bank[1][0:w, k * P:(k + 1) * P], hh[t % 2][:, k * P:k * P + w], ident)
                    mm.then_inc(m_ht, 1)

            def gate_up(t):
                with in_use(e, count, t):
                    run, _, _, at = words[t]
                    e.wait_ge(v_xt, t + 1)
                    e.wait_ge(v_gu, run + 1)
                    if t >= 2:
                        e.wait_ge(v_h, t - 1)
                    for k in range(KH):
                        hi, lo = (v[t % 2][:, k * P:(k + 1) * P] for v in (xt_hi, xt_lo))
                        for a, w, last in ((hi, w_hi, False), (hi, w_lo, False), (lo, w_hi, True)):
                            for s in range(2):
                                mm = e.matmul(bank[2 + 2 * s + t % 2][:, 0:INTER], a,
                                              w[:, bass.ds(at + (k * GU + s * INTER), INTER)],
                                              start=k == 0 and a is hi and w is w_hi,
                                              stop=k == KH - 1 and last)
                    mm.then_inc(m_gu, 1)

            def down(t):
                with in_use(e, count, t):
                    run, _, _, at = words[t]
                    e.wait_ge(v_ht, t + 1)
                    e.wait_ge(v_dn, run + 1)
                    if t >= 2:
                        e.wait_ge(a_ys, t - 1)
                    for k in range(KI):
                        n = P if k < KI - 1 else ILAST
                        hi, lo = (v[t % 2][0:n, k * P:(k + 1) * P] for v in (ht_hi, ht_lo))
                        for a, w, last in ((hi, w_hi, False), (hi, w_lo, False), (lo, w_hi, True)):
                            mm = e.matmul(bank[6 + t % 2][:], a, w[0:n, bass.ds(at + (GUW + k * H), H)],
                                          start=k == 0 and a is hi and w is w_hi, stop=k == KI - 1 and last)
                    mm.then_inc(m_dn, 1)

            words = {0: tile_word(e, 0)}
            x_turn(0)
            for t in range(NTILE + 1):
                if t >= 1:
                    h_turn(t - 1)
                if t + 1 < NTILE:
                    x_turn(t + 1)
                if t < NTILE:
                    gate_up(t)
                if t + 1 < NTILE:
                    words[t + 1] = tile_word(e, t + 1)
                if t >= 1:
                    down(t - 1)

        @blk.scalar
        def _(e):
            e.wait_ge(m_p, 1)
            e.activation(p_st[:], bank[0][:], ACT.Copy).then_inc(a_p, 1)
            e.activation(p_sb[:], bank[0][0:RR, :], ACT.Copy).then_inc(a_p, 1)
            e.wait_ge(m_qt, 1)
            e.activation(qt_sb[:], bank[1][:], ACT.Copy).then_inc(a_qt, 1)

            def x_split(b):
                e.wait_ge(d_x[b], 16)
                e.activation(x_hi[:, b], x_st[b % 2][:], ACT.Copy).then_inc(a_xhi, 1)

            def logits_out(b):
                e.wait_ge(m_lt, b + 1)
                if b >= 2:
                    e.wait_ge(m_lg, b - 1)
                e.activation(lt_sb[b % 2][:], bank[6 + b % 2][0:NEXP, :], ACT.Copy).then_inc(a_lt, 1)

            def w_split(b):
                for i in range(KH):
                    n = b * KH + i
                    e.wait_ge(v_ws, n + 1)
                    if b >= 2 and i == 0:
                        e.wait_ge(m_y, CPB * (b - 1))
                    e.activation(we_hi[b % 2][:, i], wsum[n % 2][:], ACT.Copy).then_inc(a_whi, 1)

            def y_stage(c):
                e.wait_ge(m_y, c + 1)
                if c >= 2:
                    e.wait_ge(d_y[c % 2], 16 * (c // 2))
                e.activation(y_st[c % 2][:], bank[2 + c % 2][:], ACT.Copy).then_inc(a_y, 1)

            x_split(0)
            e.wait_ge(m_g, 1)
            e.activation(gt_sb[:], bank[4][:], ACT.Copy).then_inc(a_g, 1)
            e.wait_ge(m_gt, 1)
            e.activation(g_hi[:].rearrange("p k n -> p (k n)"), bank[3][:], ACT.Copy).then_inc(a_ghi, 1)
            x_split(1)
            w_split(0)
            logits_out(0)
            x_split(2)
            w_split(1)
            logits_out(1)
            x_split(3)
            logits_out(2)
            logits_out(3)
            e.wait_ge(v_sh, 1)
            e.activation(rt[1][:], rt[0][:], ACT.Exp).then_inc(a_exp, 1)
            for c in range(CH):
                y_stage(c)
                if c == 4:
                    w_split(2)
                if c == 8:
                    w_split(3)
                if c == CH - 3:
                    count = tile_count(e)
                    split_weights(e, count, 0, None, "gu", a_gu)
                    split_weights(e, count, 0, None, "dn", a_dn)

            def x_evac(t):
                with in_use(e, count, t):
                    e.wait_ge(m_xt, t + 1)
                    if t >= 2:
                        e.wait_ge(m_gu, t - 1)
                    e.activation(xt_hi[t % 2][:], bank[0][:], ACT.Copy).then_inc(a_xt, 1)

            def h_evac(t):
                with in_use(e, count, t):
                    e.wait_ge(m_ht, t + 1)
                    if t >= 2:
                        e.wait_ge(m_dn, t - 1)
                    e.activation(ht_hi[t % 2][:], bank[1][:, 0:KI * P], ACT.Copy).then_inc(a_ht, 1)

            def silu(t):
                with in_use(e, count, t):
                    e.wait_ge(m_gu, t + 1)
                    if t >= 2:
                        e.wait_ge(v_h, t - 1)
                    e.activation(sg[t % 2][:], bank[2 + t % 2][:, 0:INTER], ACT.Silu).then_inc(a_sg, 1)

            def y_weighted(t):
                with in_use(e, count, t):
                    if t == 0:
                        e.wait_ge(v_w, 1)
                    e.wait_ge(m_dn, t + 1)
                    if t >= NYS:
                        e.wait_ge(d_s, 16 * (t - NYS + 1))
                    e.activation(ys[t % NYS][:], bank[6 + t % 2][:], ACT.Copy, scale=wtab[:, t:t + 1]).then_inc(a_ys, 1)

            x_evac(0)
            word = tile_word(e, 1)
            split_weights(e, count, 1, word, "gu", a_gu)
            split_weights(e, count, 1, word, "dn", a_dn)
            for t in range(NTILE + 1):
                if t + 2 < NTILE:
                    word = tile_word(e, t + 2)
                if t >= 1:
                    h_evac(t - 1)
                if t + 1 < NTILE:
                    x_evac(t + 1)
                if t + 2 < NTILE:
                    split_weights(e, count, t + 2, word, "gu", a_gu)
                if t < NTILE:
                    silu(t)
                if t >= 1:
                    y_weighted(t - 1)
                if t + 2 < NTILE:
                    split_weights(e, count, t + 2, word, "dn", a_dn)

        @blk.vector
        def _(e):
            done = [0]

            def step(ins):
                done[0] += 1
                ins.then_inc(v_chain, 1)
                e.wait_ge(v_chain, done[0])

            def over_e(v):
                return v.unsqueeze(2).to_broadcast([P, CH, NEXP])

            def over_c(v):
                return v.unsqueeze(1).to_broadcast([P, CH, NEXP])

            e.wait_ge(d_cst, 16)
            e.wait_ge(d_adp, 16)
            e.wait_ge(d_scl, 16)
            step(e.tensor_copy(mask[:], adp_sb[:]))
            e.tensor_scalar(mask[:], mask[:], cs[:, C_ADP:C_ADP + 1], scl_sb[:, 0:1], ALU.is_equal, ALU.mult).then_inc(v_mask, 1)
            e.wait_ge(v_mask, 1)
            e.wait_ge(a_p, 1)
            e.tensor_tensor(p_st[RR:P], bank[0][RR:P, :], p_st[RR:P], ALU.subtract).then_inc(v_plo, 1)

            def masked(b):
                if b == 0:
                    e.wait_ge(a_qt, 1)
                else:
                    if b >= 2:
                        e.wait_ge(m_we, KH * (b - 1))
                e.tensor_scalar(mq_hi[b % 2][:], qt_sb[:], mask[:, b:b + 1], None, ALU.mult).then_inc(v_mq, 1)
                e.wait_ge(v_mq, b + 1)
                e.scalar_tensor_tensor(mq_lo[b % 2][:], qt_sb[:], mask[:, b:b + 1], mq_hi[b % 2][:],
                                       ALU.mult, ALU.subtract).then_inc(v_mqlo, 1)

            def x_low(b):
                e.wait_ge(a_xhi, b + 1)
                e.tensor_tensor(x_lo[:, b], x_st[b % 2][:], x_hi[:, b], ALU.subtract).then_inc(v_xlo, 1)

            e.wait_ge(m_q, 1)
            e.tensor_copy(q_sb[:].rearrange("p k r -> p (k r)"), bank[2][:, 0:KH * RR]).then_inc(v_q, 1)
            masked(0)
            e.wait_ge(m_qg, 1)
            for b in range(NBATCH):
                for a in range(2):
                    ins = e.tensor_scalar(mqg[:, a, b], bank[3][0:RR, 0:NEXP], mask[0:RR, b:b + 1], None, ALU.mult)
            ins.then_inc(v_mqg, 1)
            masked(1)
            x_low(0)
            e.wait_ge(a_ghi, 1)
            e.tensor_tensor(g_lo[:].rearrange("p k n -> p (k n)"), bank[3][:], g_hi[:].rearrange("p k n -> p (k n)"),
                            ALU.subtract).then_inc(v_glo, 1)

            def w_sum(b):
                for i in range(KH):
                    n = b * KH + i
                    if n == 0:
                        e.wait_ge(d_wbt, 16)
                    e.wait_ge(m_we, n + 1)
                    if n >= 2:
                        e.wait_ge(p_wlo, n - 1)
                    e.tensor_tensor(wsum[n % 2][:], bank[n % 2][:], wbt_sb[:, i], ALU.add).then_inc(v_ws, 1)

            w_sum(0)
            x_low(1)
            x_low(2)
            w_sum(1)
            x_low(3)
            e.wait_ge(d_rc, 16)
            e.tensor_copy(tri[:], rc[:, R_TRI:R_TRI + P]).then_inc(v_chain, 1)
            e.tensor_copy(ones[:], rc[:, R_ONE:R_ONE + P]).then_inc(v_chain, 1)
            done[0] += 2

            sh, ex, t1, oh1, oh2, sh2, rank = rt
            mx, r1, m2, r2, sm, e1, e2, den, w1, w2, cA, cB = cc
            rev = over_c(rc[:, R_REV:R_REV + NEXP])
            e.wait_ge(m_lg, NBATCH)
            lg = bank[5][:, 0:CH * NEXP].rearrange("p (c n) -> p c n", n=NEXP)
            step(e.tensor_reduce(mx[:], lg, AX_X, ALU.max))
            e.tensor_tensor(sh[:], lg, over_e(mx[:]), ALU.subtract).then_inc(v_sh, 1)
            e.wait_ge(v_sh, 1)
            step(e.scalar_tensor_tensor(t1[:], sh[:], 0.0, rev, ALU.is_ge, ALU.mult))
            step(e.tensor_reduce(r1[:], t1[:], AX_X, ALU.max))
            step(e.tensor_tensor(oh1[:], rev, over_e(r1[:]), ALU.is_equal))
            step(e.scalar_tensor_tensor(sh2[:], oh1[:], -3.0e38, sh[:], ALU.mult, ALU.add))
            step(e.tensor_reduce(m2[:], sh2[:], AX_X, ALU.max))
            step(e.tensor_tensor(t1[:], sh2[:], over_e(m2[:]), ALU.is_equal))
            step(e.tensor_tensor(t1[:], t1[:], rev, ALU.mult))
            step(e.tensor_reduce(r2[:], t1[:], AX_X, ALU.max))
            step(e.tensor_tensor(oh2[:], rev, over_e(r2[:]), ALU.is_equal))
            e.tensor_tensor(chosen[:], oh1[:], oh2[:], ALU.add).then_inc(v_cho, 1)
            e.wait_ge(a_exp, 1)
            step(e.tensor_reduce(sm[:], ex[:], AX_X, ALU.add))
            step(e.tensor_tensor(t1[:], ex[:], oh1[:], ALU.mult))
            step(e.tensor_reduce(e1[:], t1[:], AX_X, ALU.add))
            step(e.tensor_tensor(t1[:], ex[:], oh2[:], ALU.mult))
            step(e.tensor_reduce(e2[:], t1[:], AX_X, ALU.add))
            step(e.reciprocal(cA[:], sm[:]))
            step(e.tensor_tensor(e1[:], e1[:], cA[:], ALU.mult))
            step(e.tensor_tensor(e2[:], e2[:], cA[:], ALU.mult))
            step(e.scalar_tensor_tensor(den[:], e1[:], 1e-20, e2[:], ALU.add, ALU.add))
            step(e.reciprocal(cB[:], den[:]))
            step(e.tensor_tensor(w1[:], e1[:], cB[:], ALU.mult))
            step(e.tensor_tensor(w2[:], e2[:], cB[:], ALU.mult))

            e.wait_ge(m_rk, 1)
            cnt, ntile, end, off = (v[:, 0:NEXP] for v in (sm, e1, e2, den))
            step(e.tensor_copy(cnt, bank[7][:, 0:NEXP]))
            thr = rc[:, R_THR:R_THR + 16].unsqueeze(1).to_broadcast([P, NEXP, 16])
            step(e.tensor_tensor(t1[:], cnt.unsqueeze(2).to_broadcast([P, NEXP, 16]), thr, ALU.is_gt))
            step(e.tensor_reduce(ntile, t1[:], AX_X, ALU.add))
            cum = rc[:, R_CUM:R_CUM + 256].rearrange("p (a n) -> p a n", n=NEXP)
            step(e.tensor_tensor(t1[:], ntile.unsqueeze(1).to_broadcast([P, NEXP, NEXP]), cum, ALU.mult))
            step(e.tensor_reduce(end, t1[:], AX_X, ALU.add))
            step(e.tensor_tensor(off, end, ntile, ALU.subtract))
            step(e.tensor_scalar(off, off, float(P), None, ALU.mult))
            rk = bank[6][:, 0:CH * NEXP].rearrange("p (c n) -> p c n", n=NEXP)
            step(e.tensor_tensor(rank[:], rk, over_c(off), ALU.add))
            slot = slot_f[:]
            for k, oh in enumerate((oh1, oh2)):
                step(e.tensor_tensor(t1[:], oh[:], rank[:], ALU.mult))
                step(e.tensor_reduce(slot[:, k * CH:(k + 1) * CH], t1[:], AX_X, ALU.add))
            step(e.tensor_copy(slot_i[:], slot))
            step(e.tensor_single_scalar(part_i[:], slot_i[:], P - 1, ALU.bitwise_and))
            step(e.tensor_copy(place_f[:], part_i[:]))
            step(e.tensor_single_scalar(part_i[:], slot_i[:], 7, ALU.arith_shift_right))
            step(e.tensor_copy(tile_f[:], part_i[:]))
            iqs = cs[:, C_IQ:C_IQ + TQ].unsqueeze(1).to_broadcast([P, NSEL, TQ])
            e.tensor_tensor(oh_q[:, :, 0], tile_f[:].unsqueeze(2).to_broadcast([P, NSEL, TQ]), iqs, ALU.is_equal).then_inc(v_q1, 1)

            im = rc[:, R_IM:R_IM + P].unsqueeze(1).to_broadcast([P, NSEL, P])
            e.wait_ge(v_xlo, NBATCH)
            e.tensor_tensor(oh_m[:], place_f[:].unsqueeze(2).to_broadcast([P, NSEL, P]), im, ALU.is_equal).then_inc(v_ohm, 1)
            masked(2)
            w_sum(2)

            iq = cs[0:1, C_IQ:C_IQ + TQ]
            end1, nt1 = end[0:1], ntile[0:1]
            tr = t_row[0:1]
            step(e.tensor_tensor(tr, iq.unsqueeze(2).to_broadcast([1, TQ, NEXP]),
                                 end1.unsqueeze(1).to_broadcast([1, TQ, NEXP]), ALU.is_ge))
            ef, rf, tf = (v[0:1] for v in trows)
            step(e.tensor_scalar(nt1, nt1, 0.0, None, ALU.is_gt))
            step(e.tensor_tensor(tr, tr, nt1.unsqueeze(1).to_broadcast([1, TQ, NEXP]), ALU.mult))
            step(e.tensor_reduce(rf[:, 0], tr, AX_X, ALU.add))
            step(e.tensor_scalar(rf[:, 0], rf[:, 0], float(NEXP - 1), None, ALU.min))
            step(e.memset(tf[:, 0, 0:1], 1.0))
            step(e.tensor_tensor(tf[:, 0, 1:TQ], rf[:, 0, 1:TQ], rf[:, 0, 0:TQ - 1], ALU.is_gt))
            th3 = rc[0:1, R_TH3:R_TH3 + 5]
            t3 = t_row[0:1, :, 0:5]
            step(e.tensor_tensor(t3, rf[:, 0].unsqueeze(2).to_broadcast([1, TQ, 5]),
                                 th3.unsqueeze(1).to_broadcast([1, TQ, 5]), ALU.is_ge))
            step(e.tensor_reduce(ef[:, 0], t3, AX_X, ALU.add))
            step(e.scalar_tensor_tensor(ef[:, 0], ef[:, 0], -float(NSPLIT), rf[:, 0], ALU.mult, ALU.add))
            step(e.scalar_tensor_tensor(rf[:, 0], tf[:, 0], float(W_NEW), rf[:, 0], ALU.mult, ALU.add))
            step(e.scalar_tensor_tensor(tabs[:, T_WORD], ef[:, 0], float(W_SLOT), rf[:, 0], ALU.mult, ALU.add))
            te = t_row[0:1, 0:NEXP]
            step(e.tensor_tensor(te, nt1.unsqueeze(1).to_broadcast([1, NEXP, NEXP]), cum[0:1], ALU.mult))
            step(e.tensor_reduce(ef[:, 0, 0:NEXP], te, AX_X, ALU.add))
            step(e.tensor_copy(tabs[:, T_CNT, 1:2], ef[:, 0, NEXP - 1:NEXP]))
            step(e.tensor_tensor(te, iq[:, 0:NEXP].unsqueeze(2).to_broadcast([1, NEXP, NEXP]),
                                 ef[:, 0, 0:NEXP].unsqueeze(1).to_broadcast([1, NEXP, NEXP]), ALU.is_ge))
            step(e.tensor_reduce(rf[:, 0, 0:NEXP], te, AX_X, ALU.add))
            step(e.tensor_scalar(tabs[:, T_REX, 0:NEXP], rf[:, 0, 0:NEXP], float(NEXP - 1), None, ALU.min))
            e.tensor_copy(tabs[:, T_CNT, 0:1], end[0:1, NEXP - 1:NEXP]).then_inc(v_tab, 1)

            e.wait_ge(m_tb, 1)
            step(e.tensor_scalar(tok_f[:], bank[4][:, 0:TQ], 1.0, None, ALU.subtract))
            e.tensor_copy(wtab[:], bank[4][:, TQ:2 * TQ]).then_inc(v_w, 1)
            step(e.tensor_scalar(gidx[:], tok_f[:], 0.0, None, ALU.max))
            step(e.tensor_scalar(emp_f[:], tok_f[:], 0.0, float(SKIP), ALU.is_lt, ALU.mult))
            e.tensor_tensor(sidx[:], tok_f[:], emp_f[:], ALU.add).then_inc(v_idx, 1)
            masked(3)
            w_sum(3)

            e.wait_ge(v_ws, NBATCH * KH)
            e.memset(bank[1][ILAST:P, (KI - 1) * P:KI * P], 0.0).then_inc(v_zero, 1)
            count = tile_count(e)
            split_weights(e, count, 0, None, "gu", v_gu)
            split_weights(e, count, 0, None, "dn", v_dn)

            def y_low(t):
                with in_use(e, count, t):
                    e.wait_ge(a_xt, t + 1)
                    e.tensor_tensor(xt_lo[t % 2][:], bank[0][:], xt_hi[t % 2][:], ALU.subtract).then_inc(v_xt, 1)

            def h_low(t):
                with in_use(e, count, t):
                    e.wait_ge(a_ht, t + 1)
                    e.tensor_tensor(ht_lo[t % 2][:], bank[1][:, 0:KI * P], ht_hi[t % 2][:], ALU.subtract).then_inc(v_ht, 1)

            def product(t):
                with in_use(e, count, t):
                    e.wait_ge(a_sg, t + 1)
                    if t >= 2:
                        e.wait_ge(m_ht, t - 1)
                    e.tensor_tensor(hh[t % 2][:], sg[t % 2][:], bank[4 + t % 2][:, 0:INTER], ALU.mult).then_inc(v_h, 1)

            y_low(0)
            for t in range(NTILE + 1):
                if t + 1 < NTILE:
                    word = tile_word(e, t + 1)
                if t >= 1:
                    h_low(t - 1)
                if t + 1 < NTILE:
                    y_low(t + 1)
                    split_weights(e, count, t + 1, word, "gu", v_gu)
                if t < NTILE:
                    product(t)
                if t + 1 < NTILE:
                    split_weights(e, count, t + 1, word, "dn", v_dn)

        @blk.gpsimd
        def _(e):
            def w_low(b):
                for i in range(KH):
                    n = b * KH + i
                    e.wait_ge(a_whi, n + 1)
                    e.tensor_tensor(we_lo[b % 2][:, i], wsum[n % 2][:], we_hi[b % 2][:, i], ALU.subtract).then_inc(p_wlo, 1)

            w_low(0)
            w_low(1)
            e.wait_ge(v_q1, 1)
            for k, w in enumerate((cc[8], cc[9])):
                e.tensor_tensor(oh_q[:, k * CH:(k + 1) * CH, 1], oh_q[:, k * CH:(k + 1) * CH, 0],
                                w[:].unsqueeze(2).to_broadcast([P, CH, TQ]), ALU.mult).then_inc(p_chain, 1)
            e.wait_ge(p_chain, TOPK)
            tok = cs[:, C_TOK:C_TOK + CH].unsqueeze(2).to_broadcast([P, CH, TQ])
            for k in range(TOPK):
                ins = e.tensor_tensor(oh_q[:, k * CH:(k + 1) * CH, 0], oh_q[:, k * CH:(k + 1) * CH, 0], tok, ALU.mult)
            ins.then_inc(p_ohq, 1)
            for b in (2, 3):
                w_low(b)

            count = tile_count(e)
            e.wait_ge(v_idx, 1)
            for i in range(2):
                e.wait_ge(d_y[i], 16 * (CH // 2))
            e.wait_ge(d_out, 16)

            def gather(t):
                with in_use(e, count, t):
                    if t >= NXG:
                        e.wait_ge(m_xt, t - NXG + 1)
                    e.indirect_dma_start(out=xg[t % NXG][:], out_offset=None, in_=y_dram,
                                         in_offset=bass.IndirectOffsetOnAxis(ap=gidx[:, t:t + 1], axis=0)
                                         ).then_inc(d_g[t % NXG], 16)

            def scatter(t):
                with in_use(e, count, t):
                    e.wait_ge(a_ys, t + 1)
                    if t >= 1:
                        e.wait_ge(d_s, 16 * t)
                    e.indirect_dma_start(out=out, out_offset=bass.IndirectOffsetOnAxis(ap=sidx[:, t:t + 1], axis=0),
                                         in_=ys[t % NYS][:], in_offset=None, bounds_check=NTOK - 1,
                                         oob_is_err=False, compute_op=ALU.add).then_inc(d_s, 16)
                    if t >= NFULL - 1:
                        e.wait_ge(d_s, 16 * (t + 1))

            for t in range(NXG - 1):
                gather(t)
            for t in range(NTILE):
                if t + NXG - 1 < NTILE:
                    gather(t + NXG - 1)
                scatter(t)


def kernel(**inputs):
    import numpy as np
    import concourse.bacc as bacc
    from concourse.bass_utils import run_bass_kernel_spmd

    get = {k: np.asarray(v) for k, v in inputs.items()}

    def chunks(a):
        return a.reshape(KH, P, -1).transpose(1, 0, 2)

    cst = np.zeros((P, CW), np.float32)
    cst[:, C_ID:C_ID + P] = np.eye(P)
    cst[:, C_IQ:C_IQ + TQ] = np.arange(TQ)
    cst[:, C_TOK:C_TOK + CH] = np.arange(CH) * P + np.arange(P)[:, None] + 1
    cst[:, C_ADP] = np.arange(P) % RR // RANK
    rcst = np.zeros((P, RW), np.float32)
    rcst[:, R_TRI:R_TRI + P] = np.triu(np.ones((P, P)), 1)
    rcst[:, R_ONE:R_ONE + P] = 1
    rcst[:, R_REV:R_REV + NEXP] = NEXP - np.arange(NEXP)
    rcst[:, R_THR:R_THR + 16] = P * np.arange(16)
    rcst[:, R_CUM:R_CUM + 256] = np.tril(np.ones((NEXP, NEXP))).reshape(-1)
    rcst[:, R_IM:R_IM + P] = np.arange(P)
    rcst[:, R_TH3:R_TH3 + 5] = NSPLIT * np.arange(1, 6)

    x = get["x"]
    xt = x.reshape(NBATCH, SEQ, KH, P).transpose(0, 3, 2, 1)
    at = chunks(get["L0_cond_A"].reshape(RR, H).T)
    bw = chunks(get["L0_cond_B_w"].transpose(1, 0, 2).reshape(H, RR))
    gt = chunks(get["L0_ffn_gate_w"].T)
    small = np.concatenate([at] * 2 + [bw] * 2 + [gt] * (P // NEXP), axis=2)
    adp = np.repeat(get["itok_B_0_3"][None, :], P, axis=0)
    scl = np.tile(np.repeat(get["L0_cond_scaling"], RANK), P // RR)[:, None]
    gu = np.concatenate([get[n].transpose(0, 2, 1).reshape(NEXP, KH, P, INTER) for n in ("L0_ffn_w_gate", "L0_ffn_w_up")], axis=3)
    gu = gu.transpose(0, 2, 1, 3).reshape(NEXP, P, GUW)
    dn = np.zeros((NEXP, KI * P, H), np.float32)
    dn[:, :INTER] = get["L0_ffn_w_down"].transpose(0, 2, 1)
    dn = dn.reshape(NEXP, KI, P, H).transpose(0, 2, 1, 3).reshape(NEXP, P, DW)
    arrays = {
        "cst": cst, "rcst": rcst, "small": small, "adp": adp, "scl": scl,
        "wt": chunks(get["L0_cond_Wt"]), "wpt": chunks(get["L0_cond_Wp"].T),
        "wb": chunks(get["L0_cond_W_base"]), "wbt": chunks(get["L0_cond_W_base"].T),
        "xt": xt, "x": x.reshape(NTOK, H), "wall": np.concatenate([gu, dn], axis=2),
    }
    arrays = {k: np.ascontiguousarray(v) for k, v in arrays.items()}

    nc = bacc.Bacc("TRN2", target_bir_lowering=False, num_devices=1)
    aps = {k: nc.dram_tensor(k, v.shape, mybir.dt.from_np(v.dtype), kind="ExternalInput").ap() for k, v in arrays.items()}
    out = nc.dram_tensor("out", (NTOK, H), F32, kind="ExternalOutput").ap()
    build(nc, out=out, **aps)
    r = run_bass_kernel_spmd(nc, [arrays], core_ids=[0])
    return r.results[0]["out"].reshape(NBATCH, SEQ, H)
```
